# Optimizing a Trainium2 kernel written in Bass

```python
import numpy as np
import jax
import jax.numpy as jnp

def _softmax(x, axis=-1):
    return jax.nn.softmax(x, axis=axis)

def _gelu(x):
    return jax.nn.gelu(x, approximate=True)

def _silu(x):
    return jax.nn.silu(x)

def _sigmoid(x):
    return jax.nn.sigmoid(x)

def _layernorm(x, axis=-1, eps=1e-05):
    m = jnp.mean(x, axis=axis, keepdims=True)
    v = jnp.var(x, axis=axis, keepdims=True)
    return (x - m) / jnp.sqrt(v + eps)

def _scatter_add(tgt, idx, src, axis=0):
    return tgt.at[idx].add(src)

def _segment_sum(src, seg, n):
    return jax.ops.segment_sum(src, seg, n)
kernel_name = 'mk_gnn_preln_d4_gnn_r32_b2a4b6'

def setup_inputs(seed: int=0):
    np.random.seed(seed)
    _w = jnp.asarray

    def _rec_inputs():
        import jax
        import jax.numpy as jnp
        _gk = jax.random.key(seed)
        x = -0.0003713 + 1 * jax.random.normal(jax.random.fold_in(_gk, 1), (3125, 256), jnp.float32)
        src = jax.random.randint(jax.random.fold_in(_gk, 2), (50000,), 0, 3125, jnp.int32)
        dst = jax.random.randint(jax.random.fold_in(_gk, 3), (50000,), 0, 3125, jnp.int32)
        _o = jnp.argsort(dst, stable=True)
        src = src[_o]
        dst = dst[_o]
        edge_attr_32 = jax.random.uniform(jax.random.fold_in(_gk, 11), (50000, 32), jnp.float32, 0.0, 1)
        edge_attr_64 = jax.random.uniform(jax.random.fold_in(_gk, 12), (50000, 64), jnp.float32, 0.0, 1)
        edge_type_3 = jax.random.randint(jax.random.fold_in(_gk, 14), (50000,), 0, 3, jnp.int32)
        edge_type_8 = jax.random.randint(jax.random.fold_in(_gk, 15), (50000,), 0, 8, jnp.int32)
        edge_weight = jax.random.uniform(jax.random.fold_in(_gk, 16), (50000,), jnp.float32, 0.0, 0.999998)
        return (x, src, dst, edge_attr_32, edge_attr_64, edge_type_3, edge_type_8, edge_weight)
    x, src, dst, edge_attr_32, edge_attr_64, edge_type_3, edge_type_8, edge_weight = _rec_inputs()

    def _L0_gnn_setup():
        import jax, jax.numpy as jnp
        import numpy as np
        N_NODES = 50000
        N_EDGES = 25000
        D = 256
        N_REL = 3
        N_LAYERS = 3
        N_DISTS = 32

        def _rgcn_layer(x, src, dst, edge_type, edge_attr, W, root, bias, nn_w, nn_b):
            n = x.shape[0]
            edge_w = edge_attr @ nn_w.T + nn_b
            msg = jax.nn.relu(x[src] * edge_w)
            out = x @ root + bias
            for r in range(N_REL):
                mask = edge_type == r
                m = jnp.where(mask[:, None], msg, 0.0)
                s = jax.ops.segment_sum(m, dst, num_segments=n)
                cnt = jax.ops.segment_sum(mask.astype(x.dtype), dst, num_segments=n)
                mean = s / jnp.maximum(cnt, 1.0)[:, None]
                out = out + mean @ W[r]
            return out
        key = jax.random.key(seed)
        ks = jax.random.split(key, 10)
        x = jax.random.normal(ks[0], (N_NODES, D), dtype=jnp.float32)
        edge_index = jax.random.randint(ks[1], (2, N_EDGES), 0, N_NODES)
        edge_type = jax.random.randint(ks[2], (N_EDGES,), 0, N_REL)
        edge_attr = jax.random.uniform(ks[3], (N_EDGES, N_DISTS), dtype=jnp.float32)
        W = jax.random.normal(ks[4], (N_LAYERS, N_REL, D, D), dtype=jnp.float32) * (1.0 / np.sqrt(D))
        root = jax.random.normal(ks[5], (N_LAYERS, D, D), dtype=jnp.float32) * (1.0 / np.sqrt(D))
        bias = jnp.zeros((N_LAYERS, D), dtype=jnp.float32)
        nn_w = jax.random.normal(ks[6], (D, N_DISTS), dtype=jnp.float32) * (1.0 / np.sqrt(N_DISTS))
        nn_b = jnp.zeros((D,), dtype=jnp.float32)
        return {'x': x, 'edge_index': edge_index, 'edge_type': edge_type, 'edge_attr': edge_attr, 'W': W, 'root': root, 'bias': bias, 'nn_w': nn_w, 'nn_b': nn_b}
    _L0_gnn_all = _L0_gnn_setup()
    _L0_gnn_in = {k: v for k, v in _L0_gnn_all.items() if k in ('W', 'root', 'bias', 'nn_w', 'nn_b')}
    del _L0_gnn_all

    def _L1_gnn_setup():
        import jax, jax.numpy as jnp
        import numpy as np
        N, E, HID, NRBF = (10000, 10000, 256, 64)
        key = jax.random.key(seed)
        ks = jax.random.split(key, 12)

        def lin(k, fin, fout):
            bound = 1.0 / np.sqrt(fin)
            kw, kb = jax.random.split(k)
            W = jax.random.uniform(kw, (fin, fout), jnp.float32, -bound, bound)
            b = jax.random.uniform(kb, (fout,), jnp.float32, -bound, bound)
            return (W, b)
        W1, b1 = lin(ks[0], NRBF, HID)
        W2, b2 = lin(ks[1], HID, HID)
        U1, c1 = lin(ks[2], 2 * HID, HID)
        U2, c2 = lin(ks[3], HID, HID)
        h = jax.random.normal(ks[4], (N, HID), jnp.float32)
        edge_index = jax.random.randint(ks[5], (2, E), 0, N, jnp.int64)
        rbf = jax.random.uniform(ks[6], (E, NRBF), jnp.float32)
        return {'h': h, 'edge_index': edge_index, 'rbf': rbf, 'W1': W1, 'b1': b1, 'W2': W2, 'b2': b2, 'U1': U1, 'c1': c1, 'U2': U2, 'c2': c2}
    _L1_gnn_all = _L1_gnn_setup()
    _L1_gnn_in = {k: v for k, v in _L1_gnn_all.items() if k in ('W1', 'b1', 'W2', 'b2', 'U1', 'c1', 'U2', 'c2')}
    del _L1_gnn_all

    def _L2_gnn_setup():
        import jax, jax.numpy as jnp
        import numpy as np
        N_NODES = 50000
        N_EDGES = 25000
        IN_DIM = 256
        OUT_DIM = 256
        N_REL = 8
        N_HEADS = 4
        HEAD_DIM = OUT_DIM // N_HEADS
        LEAKY_SLOPE = 0.2
        key = jax.random.key(seed)
        k1, k2, k3, k4, k5, k6 = jax.random.split(key, 6)
        x = jax.random.normal(k1, (N_NODES, IN_DIM), dtype=jnp.float32)
        W = jax.random.normal(k2, (N_REL, OUT_DIM, IN_DIM), dtype=jnp.float32) * 0.05
        a_src = jax.random.normal(k3, (N_HEADS, HEAD_DIM), dtype=jnp.float32) * 0.1
        a_dst = jax.random.normal(k4, (N_HEADS, HEAD_DIM), dtype=jnp.float32) * 0.1
        edge_index = jax.random.randint(k5, (2, N_EDGES), 0, N_NODES, dtype=jnp.int64 if jax.config.jax_enable_x64 else jnp.int32)
        edge_type = jax.random.randint(k6, (N_EDGES,), 0, N_REL, dtype=jnp.int64 if jax.config.jax_enable_x64 else jnp.int32)
        return {'x': x, 'W': W, 'a_src': a_src, 'a_dst': a_dst, 'edge_index': edge_index, 'edge_type': edge_type}
    _L2_gnn_all = _L2_gnn_setup()
    _L2_gnn_in = {k: v for k, v in _L2_gnn_all.items() if k in ('W', 'a_src', 'a_dst')}
    del _L2_gnn_all

    def _L3_gnn_setup():
        import jax, jax.numpy as jnp
        import numpy as np
        N_NODES = 50000
        N_EDGES = 25000
        H, D_IN, D_OUT = (4, 256, 64)
        key = jax.random.key(seed)
        ks = jax.random.split(key, 7)
        x = jax.random.normal(ks[0], (N_NODES, D_IN), dtype=jnp.float32)
        idx = jax.random.randint(ks[1], (2, N_EDGES), 0, N_NODES, dtype=jnp.int32)
        elem = jax.random.uniform(ks[2], (N_EDGES,), dtype=jnp.float32)
        Ws = jax.random.normal(ks[3], (H, D_IN, D_OUT), dtype=jnp.float32) * 0.05
        bs = jax.random.normal(ks[4], (H, D_OUT), dtype=jnp.float32) * 0.05
        aw = jax.random.normal(ks[5], (H, 2 * D_OUT + 1), dtype=jnp.float32) * 0.05
        ab = jax.random.normal(ks[6], (H,), dtype=jnp.float32) * 0.05
        return {'x': x, 'idx': idx, 'elem': elem, 'Ws': Ws, 'bs': bs, 'aw': aw, 'ab': ab}
    _L3_gnn_all = _L3_gnn_setup()
    _L3_gnn_in = {k: v for k, v in _L3_gnn_all.items() if k in ('Ws', 'bs', 'aw', 'ab')}
    del _L3_gnn_all
    return {'x': x, 'src': src, 'dst': dst, 'edge_attr_32': edge_attr_32, 'edge_attr_64': edge_attr_64, 'edge_type_3': edge_type_3, 'edge_type_8': edge_type_8, 'edge_weight': edge_weight, 'L0_gnn_W': _L0_gnn_in['W'], 'L0_gnn_root': _L0_gnn_in['root'], 'L0_gnn_bias': _L0_gnn_in['bias'], 'L0_gnn_nn_w': _L0_gnn_in['nn_w'], 'L0_gnn_nn_b': _L0_gnn_in['nn_b'], 'L1_gnn_W1': _L1_gnn_in['W1'], 'L1_gnn_b1': _L1_gnn_in['b1'], 'L1_gnn_W2': _L1_gnn_in['W2'], 'L1_gnn_b2': _L1_gnn_in['b2'], 'L1_gnn_U1': _L1_gnn_in['U1'], 'L1_gnn_c1': _L1_gnn_in['c1'], 'L1_gnn_U2': _L1_gnn_in['U2'], 'L1_gnn_c2': _L1_gnn_in['c2'], 'L2_gnn_W': _L2_gnn_in['W'], 'L2_gnn_a_src': _L2_gnn_in['a_src'], 'L2_gnn_a_dst': _L2_gnn_in['a_dst'], 'L3_gnn_Ws': _L3_gnn_in['Ws'], 'L3_gnn_bs': _L3_gnn_in['bs'], 'L3_gnn_aw': _L3_gnn_in['aw'], 'L3_gnn_ab': _L3_gnn_in['ab']}

def reference(x, src, dst, edge_attr_32, edge_attr_64, edge_type_3, edge_type_8, edge_weight, L0_gnn_W, L0_gnn_root, L0_gnn_bias, L0_gnn_nn_w, L0_gnn_nn_b, L1_gnn_W1, L1_gnn_b1, L1_gnn_W2, L1_gnn_b2, L1_gnn_U1, L1_gnn_c1, L1_gnn_U2, L1_gnn_c2, L2_gnn_W, L2_gnn_a_src, L2_gnn_a_dst, L3_gnn_Ws, L3_gnn_bs, L3_gnn_aw, L3_gnn_ab):
    import jax
    import jax.numpy as jnp

    def _L0_gnn_ref(x, edge_index, edge_type, edge_attr, W, root, bias, nn_w, nn_b):
        import jax, jax.numpy as jnp
        import numpy as np
        N_NODES = 50000
        N_EDGES = 25000
        D = 256
        N_REL = 3
        N_LAYERS = 3
        N_DISTS = 32

        def _rgcn_layer(x, src, dst, edge_type, edge_attr, W, root, bias, nn_w, nn_b):
            n = x.shape[0]
            edge_w = edge_attr @ nn_w.T + nn_b
            msg = jax.nn.relu(x[src] * edge_w)
            out = x @ root + bias
            for r in range(N_REL):
                mask = edge_type == r
                m = jnp.where(mask[:, None], msg, 0.0)
                s = jax.ops.segment_sum(m, dst, num_segments=n)
                cnt = jax.ops.segment_sum(mask.astype(x.dtype), dst, num_segments=n)
                mean = s / jnp.maximum(cnt, 1.0)[:, None]
                out = out + mean @ W[r]
            return out
        src, dst = (edge_index[0], edge_index[1])
        h = x
        for l in range(N_LAYERS):
            h = _rgcn_layer(h, src, dst, edge_type, edge_attr, W[l], root[l], bias[l], nn_w, nn_b)
        return h

    def _L1_gnn_ref(h, edge_index, rbf, W1, b1, W2, b2, U1, c1, U2, c2):
        import jax, jax.numpy as jnp
        import numpy as np
        N, E, HID, NRBF = (10000, 10000, 256, 64)
        src, dst = (edge_index[0], edge_index[1])
        gate = jax.nn.sigmoid(jax.nn.silu(rbf @ W1 + b1) @ W2 + b2)
        msg = gate * h[src]
        aggr = jax.ops.segment_sum(msg, dst, num_segments=h.shape[0])
        upd = jax.nn.silu(jnp.concatenate([h, aggr], axis=-1) @ U1 + c1) @ U2 + c2
        return h + upd

    def _L2_gnn_ref(x, W, a_src, a_dst, edge_index, edge_type):
        import jax, jax.numpy as jnp
        import numpy as np
        N_NODES = 50000
        N_EDGES = 25000
        IN_DIM = 256
        OUT_DIM = 256
        N_REL = 8
        N_HEADS = 4
        HEAD_DIM = OUT_DIM // N_HEADS
        LEAKY_SLOPE = 0.2
        num_nodes = x.shape[0]
        h_stack = jnp.einsum('ni,rdi->rnd', x, W)
        src, dst = (edge_index[0], edge_index[1])
        h_src = h_stack[edge_type, src].reshape(-1, N_HEADS, HEAD_DIM)
        h_dst = h_stack[edge_type, dst].reshape(-1, N_HEADS, HEAD_DIM)
        attn_src = jnp.sum(h_src * a_src, axis=-1)
        attn_dst = jnp.sum(h_dst * a_dst, axis=-1)
        attn = jax.nn.leaky_relu(attn_src + attn_dst, negative_slope=LEAKY_SLOPE)
        attn = jax.nn.softmax(attn, axis=0)
        msg = (h_src * attn[:, :, None]).reshape(-1, OUT_DIM)
        out = jax.ops.segment_sum(msg, dst, num_segments=num_nodes)
        return out

    def _L3_gnn_ref(x, idx, elem, Ws, bs, aw, ab):
        import jax, jax.numpy as jnp
        import numpy as np
        N_NODES = 50000
        N_EDGES = 25000
        H, D_IN, D_OUT = (4, 256, 64)
        N = x.shape[0]
        O = Ws.shape[-1]
        feats = jnp.einsum('nd,hdo->hno', x, Ws) + bs[:, None, :]
        aw_src, aw_dst, aw_e = (aw[:, :O], aw[:, O:2 * O], aw[:, 2 * O])
        a_s = jnp.einsum('hno,ho->hn', feats, aw_src)
        a_d = jnp.einsum('hno,ho->hn', feats, aw_dst)
        src, dst = (idx[0], idx[1])
        score = a_s[:, src] + a_d[:, dst] + aw_e[:, None] * elem[None, :] + ab[:, None]
        w = jnp.exp(-jax.nn.relu(score / 20.0))
        dst_f = feats[:, dst]
        seg = lambda vals: jax.ops.segment_sum(vals, src, num_segments=N)
        pooled = jax.vmap(lambda wi, fi: seg(wi[:, None] * fi))(w, dst_f)
        row_sum = jax.vmap(lambda wi: seg(wi))(w)
        out = pooled / row_sum[:, :, None]
        return jnp.transpose(out, (1, 0, 2)).reshape(N, H * O)
    edge_index = jnp.stack([src, dst])
    h = jnp.maximum(_layernorm(x, axis=-1), 0.0)
    x = x + _L0_gnn_ref(h, edge_index, edge_type_3, edge_attr_32, L0_gnn_W, L0_gnn_root, L0_gnn_bias, L0_gnn_nn_w, L0_gnn_nn_b)
    h = jnp.maximum(_layernorm(x, axis=-1), 0.0)
    x = x + _L1_gnn_ref(h, edge_index, edge_attr_64, L1_gnn_W1, L1_gnn_b1, L1_gnn_W2, L1_gnn_b2, L1_gnn_U1, L1_gnn_c1, L1_gnn_U2, L1_gnn_c2)
    h = jnp.maximum(_layernorm(x, axis=-1), 0.0)
    x = x + _L2_gnn_ref(h, L2_gnn_W, L2_gnn_a_src, L2_gnn_a_dst, edge_index, edge_type_8)
    h = jnp.maximum(_layernorm(x, axis=-1), 0.0)
    x = x + _L3_gnn_ref(h, edge_index, edge_weight, L3_gnn_Ws, L3_gnn_bs, L3_gnn_aw, L3_gnn_ab)
    return x

_drawn_inputs = setup_inputs


def setup_inputs(seed=0):
    import zlib

    import numpy as np

    out = dict(_drawn_inputs(seed))
    spreads = {'L0_gnn_bias': (0.0, 0.1), 'L0_gnn_nn_b': (0.0, 0.1)}
    factors = {'edge_attr_64': 8.0,
     'edge_weight': 64.0,
     'L1_gnn_W1': 4.191,
     'L1_gnn_b1': 25.339,
     'L1_gnn_W2': 4.133,
     'L1_gnn_b2': 64.0,
     'L1_gnn_c1': 8.0,
     'L1_gnn_c2': 3.189,
     'L2_gnn_W': 8.0,
     'L2_gnn_a_src': 8.0,
     'L2_gnn_a_dst': 8.0,
     'L3_gnn_aw': 64.0,
     'L3_gnn_ab': 64.0}
    for name, (base, spread) in spreads.items():
        noise = np.random.default_rng([zlib.crc32(name.encode()), seed]).standard_normal(out[name].shape)
        drawn = base * np.exp(spread * noise) if base else spread * noise
        out[name] = jnp.asarray(drawn.astype(out[name].dtype))
    for name, factor in factors.items():
        out[name] = (out[name] * factor).astype(out[name].dtype)
    return out
```

```python
from contextlib import ExitStack

import concourse.bass as bass
from concourse import mybir

F32 = mybir.dt.float32
BF16 = mybir.dt.bfloat16
I32 = mybir.dt.int32
ALU = mybir.AluOpType
ACT = mybir.ActivationFunctionType
AX = mybir.AxisListType

P = 128
N, D, E = 3125, 256, 50000
DH = D // P
T = -(-N // P)
NP = T * P
NLAST = N - (T - 1) * P
R3, R8 = 3, 8
NH, HD = 4, D // 4
A32, A64 = 32, 64
KD = T * R3
KS = T
K = KD + KS
U = 18
HU = U // 2
QU = 3
RING, BANKS = 6, 3
U3, Q3 = 20, 5
TG = 5
CREDIT = 24


def round_up(a, b):
    return -(-a // b) * b


NC1 = round_up((E + (P - 1) * KD) // P, U)
NC2 = round_up((E + (P - 1) * KS) // P, U3)
TURNS1, TURNS2 = NC1 // U, NC2 // U3
SG = 4
EC = round_up(-(-E // P), 2 * SG)
ELAST = E - (P - 1) * EC
NMETA = 4
WMETA, WA32 = D, D + NMETA
REC = WA32 + A32
SPARE = NC1 - -(-E // P)
EMPTY2 = NC2 // 3
LASTS = 5
G2, GROUPS2 = 2, 4
REC2 = 3
EPS = 1e-5
NEG = -1e30


class Chain:

    def __init__(self, eng, sem):
        self.eng, self.sem, self.n = eng, sem, 0

    def __call__(self, ins):
        self.n += 1
        ins.then_inc(self.sem, 1)
        self.eng.wait_ge(self.sem, self.n)


def wait_ahead(eng, *waits):
    waits = [(s, eng.to_reg(n)) for s, n in waits]
    eng.wait_ge(waits[0][0], 1)
    for s, n in waits:
        eng.wait_ge(s, n)


def upto(n):
    return n + 1 + CREDIT


def walk(eng, turns, *lags, width=U):
    def at(i, s, lag, first, last):
        if s >= lag:
            return None if last else (i * width + (s - lag), i, s - lag)
        return None if first else (i * width + (s - lag), i - 1, s - lag + width)

    for s in range(width):
        yield [at(0, s, lag, True, False) for lag in lags]
    with eng.Fori(1, turns) as i:
        for s in range(width):
            yield [at(i, s, lag, False, False) for lag in lags]
    for s in range(max(lags)):
        yield [at(turns, s, lag, False, True) for lag in lags]


class Buckets:

    def __init__(self, nc, engine, table, most, lag, width=U, part=QU):
        self.nc, self.engine, self.table, self.most, self.lag, self.width, self.part = nc, engine, table, most, lag, width, part
        self.values = []

    def __call__(self, chunk):
        n, _, s = chunk
        step = (s + self.lag) % self.width
        first = isinstance(n, int) and n == 0
        if first or step % self.part == 0:
            count = self.part - step % self.part
            if isinstance(n, int) and not first and n >= self.width:
                count = min(count, self.lag - step)
            _, self.values = self.nc.values_load_multi_w_load_instructions(
                self.table[:, ds(n, count)], engines=[self.engine], min_val=0, max_val=self.most)
            self.values = list(self.values)
        return self.values.pop(0)


def tiles(eng):
    with eng.Fori(0, T // 2) as i:
        yield i * 2, 0
        yield i * 2 + 1, 1
    yield T - 1, 0


def since(s):
    return 1 if s == 0 else 2


def ds(a, n=1):
    return bass.ds(a, n)


def build(nc, x, src, dst, edge_attr_32, edge_attr_64, edge_type_3, edge_type_8, edge_weight,
          L0_gnn_W, L0_gnn_root, L0_gnn_bias, L0_gnn_nn_w, L0_gnn_nn_b,
          L1_gnn_W1, L1_gnn_b1, L1_gnn_W2, L1_gnn_b2, L1_gnn_U1, L1_gnn_c1, L1_gnn_U2, L1_gnn_c2,
          L2_gnn_W, L2_gnn_a_src, L2_gnn_a_dst, L3_gnn_Ws, L3_gnn_bs, L3_gnn_aw, L3_gnn_ab, out):
    top = ExitStack()
    used_sems = {}

    def sem(name):
        if name not in used_sems:
            used_sems[name] = top.enter_context(nc.semaphore(name))
        return used_sems[name]

    taken = {}

    def unique(name):
        taken[name] = taken.get(name, 0) + 1
        return name if taken[name] == 1 else f"{name}_{taken[name]}"

    def sb(ctx, name, shape, dt=F32):
        return ctx.enter_context(nc.sbuf_tensor(unique(name), shape, dt))

    def ps(ctx, name, shape, dt=F32):
        return ctx.enter_context(nc.psum_tensor(unique(name), shape, dt))

    def clear_semaphores():
        with nc.Block() as block:
            @block.gpsimd
            def _(pool):
                for name, s in used_sems.items():
                    if not name.startswith("sw_") and name != "emptied":
                        pool.sem_clear(s)

    def dram(name, shape, dt=F32):
        return nc.dram_tensor(name, shape, dt).ap()

    rec_d = dram("rec_dram", (NC1 * P + EC, REC))
    rec2_d = dram("rec2_dram", (NC2 * P + EC, REC2))
    h_d = dram("h_dram", (NP, D))
    attT_d = dram("attT_dram", (A32, NC1, P))
    rel_d = dram("rel_dram", (R8 * NP, D))
    relatt_d = dram("relatt_dram", (R8 * NP, NH))
    feat_d = dram("feat_dram", (NP, D + 2 * NH))

    with top:
        X = sb(top, "X", [P, T, D])
        hT = sb(top, "hT", [P, T, DH, P])
        arena = sb(top, "arena", [P, KD * D])
        iota = sb(top, "iota", [P, 512])
        pcol = sb(top, "pcol", [P, 1])
        ident = sb(top, "ident", [P, P])
        identb = sb(top, "identb", [P, P], BF16)
        ones = sb(top, "ones", [P, P])
        inv_cnt = sb(top, "inv_cnt", [P, KD])
        bmap = sb(top, "bmap", [1, 3, NC1], I32)
        meta = sb(top, "meta", [P, NC1, NMETA])
        idx = sb(top, "idx", [P, 2, NC1], I32)
        rows2 = sb(top, "rows2", [P, EC, REC2])
        place2 = sb(top, "place2", [P, EC], I32)
        now2 = sb(top, "now2", [P, GROUPS2, G2, REC2])
        to2 = sb(top, "to2", [P, GROUPS2, G2], I32)

        def credit(eng, *names):
            for name in names:
                eng.sem_inc(sem(name), CREDIT)

        def sort_edges():
            ctx = ExitStack()
            with ctx:
                a = [0]

                def area(n):
                    a[0] += n
                    return arena[:, a[0] - n:a[0]]
                ints = area(4 * EC).bitcast(I32).rearrange("p (f c) -> p f c", f=4)
                dst_i, src_i, t3_i, t8_i = (ints[:, f, :] for f in range(4))
                tmp_i = area(4 * EC).bitcast(I32).rearrange("p (f c) -> p f c", f=4)
                key_d, key_s = area(EC), area(EC)
                trash1, trash2 = area(EC), area(EC)
                m1 = area(NMETA * EC).rearrange("p (f c) -> p f c", f=NMETA)
                weight = area(EC)
                pcol_i = sb(ctx, "pcol_i", [P, 1], I32)
                lt = sb(ctx, "lt", [P, P])
                ltk = sb(ctx, "ltk", [P, P])
                sel = sb(ctx, "sel", [P, 3])
                tile_end = sb(ctx, "tile_end", [P, T])
                zerob = sb(ctx, "zerob", [P, P], BF16)
                empty = sb(ctx, "empty", [P, REC])
                last_chunk = sb(ctx, "last_chunk", [1, KD], I32)
                empty2 = sb(ctx, "empty2", [P, EMPTY2, REC2])
                small = sb(ctx, "small", [P, 8])
                small_i = sb(ctx, "small_i", [P, 2], I32)
                hist = sb(ctx, "hist", [P, K])
                base = sb(ctx, "base", [P, K])
                ended = sb(ctx, "ended", [P, NC1])
                OK = sb(ctx, "OK", [P, 2, SG, K], BF16)
                OL = sb(ctx, "OL", [P, 2, SG, P], BF16)
                prod = sb(ctx, "prod", [P, 2, SG, K])
                posf = sb(ctx, "posf", [P, 2, 2, SG])
                pos = sb(ctx, "pos", [P, 2, SG], I32)
                at32 = sb(ctx, "at32", [P, 2, SG, A32])
                at64 = sb(ctx, "at64", [P, 2, SG, A64])
                rec = sb(ctx, "rec", [P, 2, SG, REC])
                W1 = sb(ctx, "W1", [P, D])
                W2 = sb(ctx, "W2", [P, DH, D])
                b2 = sb(ctx, "b2", [P, D])
                b2rest = sb(ctx, "b2rest", [P, D])
                b2part = sb(ctx, "b2part", [P, D], BF16)
                b2b = sb(ctx, "b2b", [P, D], BF16)
                onesb = sb(ctx, "onesb", [P, P], BF16)
                aT = sb(ctx, "aT", [P, 2, P])
                sig = sb(ctx, "sig", [P, 2, D])
                silu = sb(ctx, "silu", [P, 4, D])
                pctx = ExitStack()
                ps_h = ps(pctx, "ps_h", [P, K])
                ps_c = ps(pctx, "ps_c", [P, KD])
                ps_s = ps(pctx, "ps_s", [P, 2])
                ps_m = [ps(pctx, f"ps_m{m}", [P, NC1]) for m in range(3)]
                ps_l = ps(pctx, "ps_l", [P, KD])

                def edges(sp, to, of, s):
                    sp.dma_start(to[0:112, :], of[0:112 * EC].rearrange("(p c) -> p c", c=EC)).then_inc(s, 16)
                    sp.dma_start(to[112:P - 1, :],
                                 of[112 * EC:(P - 1) * EC].rearrange("(p c) -> p c", c=EC)).then_inc(s, 16)
                    sp.dma_start(to[P - 1:P, 0:ELAST],
                                 of[(P - 1) * EC:E].rearrange("(p c) -> p c", p=1)).then_inc(s, 16)

                with nc.Block() as block:
                    @block.sync
                    def _(sp):
                        sp.wait_ge(sem("preset"), 2)
                        for to, of in ((dst_i, dst), (src_i, src), (t3_i, edge_type_3), (t8_i, edge_type_8)):
                            edges(sp, to, of, sem("ints_in"))
                        edges(sp, weight, edge_weight, sem("ints_in"))
                        sp.wait_ge(sem("preset"), 3)
                        sp.dma_start(W1[0:A64, :], L1_gnn_W1).then_inc(sem("w_in"), 16)
                        sp.dma_start(W1[A64:A64 + 1, :], L1_gnn_b1.rearrange("(a d) -> a d", a=1)).then_inc(sem("w_in"), 16)
                        sp.dma_start(W2[:], L1_gnn_W2.rearrange("(h p) d -> p h d", p=P)).then_inc(sem("w_in"), 16)
                        for q in range(3):
                            sp.dma_start(b2[32 * q:32 * q + 1, :], L1_gnn_b2.rearrange("(a d) -> a d", a=1)).then_inc(sem("w_in"), 16)
                        sp.dma_start(X[:, 0:T - 1, :],
                                     x[0:(T - 1) * P, :].rearrange("(t p) d -> p t d", p=P)).then_inc(sem("x_in"), 16)
                        sp.dma_start(X[0:NLAST, T - 1, :], x[(T - 1) * P:N, :]).then_inc(sem("x_in"), 16)
                        sp.wait_ge(sem("empty_set"), 1)
                        sp.dma_start(rec_d[(NC1 - SPARE) * P:NC1 * P, :].rearrange("(p j) w -> p j w", p=P),
                                     empty[:].unsqueeze(1).to_broadcast([P, SPARE, REC])).then_inc(sem("emptied"), 16)
                        rows2_d = rec2_d[0:NC2 * P, :].rearrange("(p j) w -> p j w", p=P)
                        for j in range(0, NC2, EMPTY2):
                            sp.dma_start(rows2_d[:, j:j + EMPTY2, :], empty2[:]).then_inc(sem("emptied"), 16)
                        sp.wait_ge(sem("x_in"), 32)
                        sp.wait_ge(sem("w_in"), 16 * 6)

                    @block.gpsimd
                    def _(pool):
                        nc.gpsimd.iota(iota[:], [[1, 512]], base=0, channel_multiplier=0,
                                       allow_small_or_imprecise_dtypes=True).then_inc(sem("iotas"), 1)
                        nc.gpsimd.iota(pcol[:], [[1, 1]], base=0, channel_multiplier=1,
                                       allow_small_or_imprecise_dtypes=True).then_inc(sem("iotas"), 1)
                        nc.gpsimd.iota(tile_end[:], [[R3, T]], base=R3 - 1, channel_multiplier=0,
                                       allow_small_or_imprecise_dtypes=True).then_inc(sem("iotas"), 1)

                    @block.vector
                    def _(dve):
                        v = nc.vector
                        v.memset(ints[:, :, ELAST:EC], -1).then_inc(sem("preset"), 1)
                        v.memset(weight[:, ELAST:EC], 0.0)
                        v.memset(X[:, T - 1, :], 0.0).then_inc(sem("preset"), 1)
                        step = Chain(dve, sem("chain"))
                        v.memset(ones[:], 1.0)
                        v.memset(zerob[:], 0.0)
                        v.memset(at32[:], 0.0)
                        v.memset(at64[:], 0.0)
                        v.memset(W1[:], 0.0)
                        v.memset(b2[:], 0.0).then_inc(sem("preset"), 1)
                        v.memset(b2b[:], 0.0)
                        v.memset(onesb[:], 1.0)
                        step(v.memset(aT[:], 0.0))
                        v.memset(aT[A64:A64 + 1, :, :], 1.0)
                        v.memset(empty[:], 0.0)
                        step(v.memset(empty2[:], 0.0))
                        v.memset(empty2[:, :, 0:1], -1.0)
                        v.memset(empty[:, WMETA:WMETA + 1], -1.0).then_inc(sem("empty_set"), 1)
                        dve.wait_ge(sem("iotas"), 3)
                        v.tensor_scalar(ident[:], iota[:, 0:P], pcol[:], None, ALU.is_equal)
                        v.tensor_scalar(identb[:], iota[:, 0:P], pcol[:], None, ALU.is_equal)
                        v.tensor_scalar(sel[:, 0:1], pcol[:], float(KD), None, ALU.is_lt)
                        v.tensor_scalar(small[:, 0:1], pcol[:], float(KD), None, ALU.is_ge)
                        step(v.tensor_scalar(tile_end[:], tile_end[:], pcol[:], None, ALU.is_equal))
                        v.tensor_reduce(sel[:, 1:2], tile_end[:], AX.X, ALU.add)
                        v.tensor_scalar(sel[:, 2:3], pcol[:], float(K), small[:, 0:1], ALU.is_lt, ALU.mult)
                        v.tensor_scalar(lt[:], iota[:, 0:P], pcol[:], None, ALU.is_gt)
                        step(v.tensor_scalar(ltk[:], iota[:, 0:P], float(KD), sel[:, 0:1], ALU.is_ge, ALU.mult))
                        step(v.tensor_tensor(ltk[:], lt[:], ltk[:], ALU.subtract))
                        dve.wait_ge(sem("ints_in"), 16 * 15)
                        for f, (of, op, by) in enumerate(((dst_i, ALU.arith_shift_right, 7), (dst_i, ALU.bitwise_and, 127),
                                                          (src_i, ALU.arith_shift_right, 7), (src_i, ALU.bitwise_and, 127))):
                            last = v.tensor_scalar(tmp_i[:, f, :], of, by, None, op)
                        step(last)
                        v.scalar_tensor_tensor(key_d, tmp_i[:, 0, :], float(R3), t3_i, ALU.mult, ALU.add)
                        v.tensor_scalar(key_s, tmp_i[:, 2, :], float(KD), None, ALU.add)
                        v.tensor_copy(m1[:, 0, :], tmp_i[:, 1, :])
                        v.tensor_copy(m1[:, 1, :], src_i)
                        v.scalar_tensor_tensor(m1[:, 2, :], t8_i, float(NP), src_i, ALU.mult, ALU.add)
                        v.tensor_copy(m1[:, 3, :], t8_i)
                        v.tensor_copy(rows2[:, :, 0], tmp_i[:, 3, :])
                        v.tensor_copy(rows2[:, :, 2], weight)
                        v.tensor_scalar(trash1, iota[:, 0:EC], float(NC1 * P), None, ALU.add)
                        v.tensor_scalar(trash2, iota[:, 0:EC], float(NC2 * P), None, ALU.add)
                        step(v.tensor_copy(rows2[:, :, 1], dst_i))
                        v.scalar_tensor_tensor(trash1, key_d, 0.0, trash1, ALU.is_lt, ALU.mult)
                        step(v.scalar_tensor_tensor(trash2, key_d, 0.0, trash2, ALU.is_lt, ALU.mult))
                        dve.wait_ge(sem("w_in"), 16 * 6)
                        for q in range(3):
                            step(v.tensor_copy(b2part[:], b2[:] if q == 0 else b2rest[:]))
                            v.tensor_copy(b2b[32 * q:32 * q + 1, :], b2part[32 * q:32 * q + 1, :])
                            step(v.tensor_tensor(b2rest[:], b2[:] if q == 0 else b2rest[:], b2part[:], ALU.subtract))
                clear_semaphores()

                def one_hot_keys(g, b):
                    cols = ds(g * SG, SG)
                    nc.vector.tensor_tensor(OK[:, b, :, 0:KD], key_d[:, cols].unsqueeze(2).to_broadcast([P, SG, KD]),
                                            iota[:, 0:KD].unsqueeze(1).to_broadcast([P, SG, KD]), ALU.is_equal)
                    return nc.vector.tensor_tensor(OK[:, b, :, KD:K], key_s[:, cols].unsqueeze(2).to_broadcast([P, SG, KS]),
                                                   iota[:, KD:K].unsqueeze(1).to_broadcast([P, SG, KS]), ALU.is_equal)

                NG = EC // SG
                def empty_last_chunks(eng, engine, first, count):
                    eng.wait_ge(sem("emptied"), 16 * (1 + NC2 // EMPTY2))
                    eng.wait_ge(sem("lasts"), 1)
                    with eng.Fori(0, count // LASTS) as i:
                        _, chunks = nc.values_load_multi_w_load_instructions(
                            last_chunk[0:1, ds(first + i * LASTS, LASTS)], engines=[engine], min_val=0, max_val=NC1 - 1)
                        for c in chunks:
                            eng.dma_start(rec_d[ds(c * P, P), :], empty[:]).then_inc(sem("emptied"), 16)

                with nc.Block() as block:
                    @block.sync
                    def _(sp):
                        empty_last_chunks(nc.sync, mybir.EngineType.SP, 0, 40)

                    @block.scalar
                    def _(act):
                        empty_last_chunks(nc.scalar, mybir.EngineType.Activation, 40, KD - 40)

                    @block.vector
                    def _(dve):
                        dve.sem_inc(sem("counted"), 2)
                        with nc.vector.Fori(0, NG // 2) as i:
                            for b in range(2):
                                g = i * 2 + b
                                dve.wait_ge(sem("counted"), g + 1)
                                one_hot_keys(g, b)
                                nc.vector.tensor_tensor(
                                    OL[:, b, :, :], m1[:, 0, ds(g * SG, SG)].unsqueeze(2).to_broadcast([P, SG, P]),
                                    iota[:, 0:P].unsqueeze(1).to_broadcast([P, SG, P]), ALU.is_equal).then_inc(sem("hot"), 1)
                        dve.wait_ge(sem("totals"), 1)
                        v, step = nc.vector, Chain(dve, sem("chain"))
                        v.tensor_copy(hist[:], ps_h[:]).then_inc(sem("hist"), 1)
                        step(v.tensor_scalar(inv_cnt[:], ps_c[:], 1.0, None, ALU.max))
                        v.reciprocal(inv_cnt[:], inv_cnt[:])
                        dve.wait_ge(sem("totals"), 2)
                        step(v.tensor_scalar(small_i[0:K, 0:1], ps_s[0:K, 0:1], float(P - 1), None, ALU.add))
                        step(v.tensor_scalar(small_i[0:K, 1:2], small_i[0:K, 0:1], 7, None, ALU.arith_shift_right))
                        v.tensor_copy(small[0:K, 3:4], small_i[0:K, 1:2]).then_inc(sem("chunks"), 1)
                        dve.wait_ge(sem("totals"), 3)
                        step(v.tensor_copy(small[0:K, 4:5], ps_s[0:K, 1:2]))
                        step(v.tensor_tensor(small[0:K, 5:6], small[0:K, 4:5], small[0:K, 3:4], ALU.add))
                        v.tensor_scalar(base[0:K, :], ident[0:K, 0:K], small[0:K, 4:5], float(P), ALU.mult, ALU.mult)
                        v.tensor_scalar(ended[0:K, :], iota[0:K, 0:NC1], small[0:K, 5:6], None,
                                        ALU.is_ge).then_inc(sem("ended"), 1)
                        dve.wait_ge(sem("ends"), 1)
                        v.tensor_scalar(last_chunk[:], ps_l[0:1, :], -1.0, 0.0, ALU.add, ALU.max).then_inc(sem("lasts"), 1)
                        dve.wait_ge(sem("totals"), 4)
                        for m, most in enumerate((KD - 1, T - 1, T - 1)):
                            last = v.tensor_scalar(bmap[0:1, m, :], ps_m[m][0:1, :], float(most), None, ALU.min)
                        step(last)

                    @block.tensor
                    def _(pe):
                        t = nc.tensor
                        t.matmul(ps_h[:], zerob[:], identb[:, 0:K], start=True, stop=False)
                        t.matmul(ps_c[:], zerob[:], identb[:, 0:KD], start=True, stop=False)
                        with nc.tensor.Fori(0, NG // 2) as i:
                            for b in range(2):
                                pe.wait_ge(sem("hot"), i * 2 + b + 1)
                                for j in range(SG):
                                    t.matmul(ps_h[:], identb[:], OK[:, b, j, :], start=False, stop=False)
                                    last = t.matmul(ps_c[:], OL[:, b, j, :], OK[:, b, j, 0:KD], start=False, stop=False)
                                last.then_inc(sem("counted"), 1)
                        t.matmul(ps_h[:], zerob[:], identb[:, 0:K], start=False, stop=True)
                        t.matmul(ps_c[:], zerob[:], identb[:, 0:KD], start=False, stop=True).then_inc(sem("totals"), 1)
                        pe.wait_ge(sem("hist"), 1)
                        t.matmul(ps_s[0:K, 0:1], hist[:], ones[:, 0:1], start=True, stop=True).then_inc(sem("totals"), 1)
                        pe.wait_ge(sem("chunks"), 1)
                        t.matmul(ps_s[0:K, 1:2], ltk[0:K, 0:K], small[0:K, 3:4], start=True, stop=True).then_inc(sem("totals"), 1)
                        pe.wait_ge(sem("ended"), 1)
                        t.matmul(ps_l[0:1, :], small[0:K, 5:6], ident[0:K, 0:KD], start=True, stop=True).then_inc(sem("ends"), 1)
                        for m in range(3):
                            last = t.matmul(ps_m[m][0:1, :], sel[0:K, m:m + 1], ended[0:K, :], start=True, stop=True)
                        last.then_inc(sem("totals"), 1)
                clear_semaphores()

                pctx.close()
                FULL = ELAST // (2 * SG)
                OUTS = 16
                SW = 2 * SG
                pctx = ExitStack()
                ps_r = ps(pctx, "ps_r", [P, SG, K])
                ps_t = [ps(pctx, f"ps_t{b}", [A64, P]) for b in range(2)]
                ps_z = [ps(pctx, f"ps_z{b}", [P, DH, P]) for b in range(2)]
                ps_g = [ps(pctx, f"ps_g{b}", [P, D]) for b in range(2)]
                with nc.Block() as block:
                    @block.sync
                    def _(sp):
                        def load(i, parts):
                            for b in range(2):
                                g = i * 2 + b
                                wait_ahead(sp, (sem("aT"), upto(g * SG + SG - 1 - 2 * SG)), (sem("a32"), upto(g - 2)))
                                for to, of, w in ((at32, edge_attr_32, A32), (at64, edge_attr_64, A64)):
                                    for lo, hi in parts:
                                        src_ap = bass.AP(tensor=of.tensor, offset=(g * SG + lo * EC) * w,
                                                         ap=[[EC * w, hi - lo], [1, SG * w]])
                                        sp.dma_start(to[lo:hi, b, :, :].rearrange("p c w -> p (c w)"),
                                                     src_ap).then_inc(sem(f"attr_in{b}"), 16)
                        with nc.sync.Fori(0, FULL) as i:
                            load(i, ((0, 112), (112, P)))
                        with nc.sync.Fori(FULL, NG // 2) as i:
                            load(i, ((0, 112), (112, P - 1)))

                    @block.scalar
                    def _(act):
                        credit(act, "a32", "aT_sb", "sig", "gate")
                        for c0, c1, c3 in walk(nc.scalar, NG // 2, 0, 2, 4, width=SW):
                            if c0:
                                n, i, s = c0
                                b = s // SG
                                act.wait_ge(sem("aT"), upto(n))
                                act.wait_ge(sem("z"), upto(n - 2))
                                nc.scalar.copy(aT[0:A64, s % 2, :], ps_t[s % 2][:]).then_inc(sem("aT_sb"), 1)
                            if c1:
                                n, i, s = c1
                                act.wait_ge(sem("z"), upto(n))
                                act.wait_ge(sem("silu"), upto(n - 2))
                                nc.scalar.activation(sig[:, s % 2, :], ps_z[s % 2][:].rearrange("p h e -> p (h e)"),
                                                     ACT.Sigmoid).then_inc(sem("sig"), 1)
                            if c3:
                                n, i, s = c3
                                act.wait_ge(sem("g"), upto(n))
                                if not isinstance(i, int) or i > 0:
                                    act.wait_ge(sem(f"sw_rec{s}"), i * OUTS)
                                nc.scalar.activation(rec[:, s // SG, s % SG, 0:D], ps_g[s % 2][:], ACT.Sigmoid).then_inc(sem("gate"), 1)
                            if c0:
                                n, i, s = c0
                                b = s // SG
                                if s % SG == 3:
                                    if not isinstance(i, int):
                                        for j in range(SG):
                                            act.wait_ge(sem(f"sw_rec{b * SG + j}"), i * OUTS)
                                    nc.scalar.copy(rec[:, b, :, WA32:WA32 + A32], at32[:, b, :, :]).then_inc(sem("a32"), 1)

                    @block.tensor
                    def _(pe):
                        t = nc.tensor

                        def four(of, n=SG):
                            return of.unsqueeze(1).to_broadcast([of.shape[0], n, K])
                        credit(pe, "aT", "z", "g")
                        t.matmul(ps_r[:], lt[:], four(hist[:]), start=True, stop=False)
                        t.matmul(ps_r[:], ones[0:K, :], four(base[0:K, :]), start=False, stop=True)
                        for c0, c1, c3 in walk(nc.tensor, NG // 2, 0, 1, 4, width=SW):
                            if c0:
                                n, i, s = c0
                                b, j = s // SG, s % SG
                                waits = [(sem("aT_sb"), upto(n - 2))]
                                if j == 0:
                                    waits.append((sem(f"attr_in{b}"), i * 64 + 64))
                                wait_ahead(pe, *waits)
                                t.transpose(ps_t[s % 2][:], at64[:, b, j, :], ident[:]).then_inc(sem("aT"), 1)
                                if j == 0:
                                    pe.wait_ge(sem("hot"), i * 2 + b + 1)
                                    for j in range(SG - 1):
                                        last = t.matmul(ps_r[:, j + 1:SG, :], identb[:], four(OK[:, b, j, :], SG - 1 - j),
                                                        start=False, stop=(j == SG - 2), skip_group_check=True)
                                    last.then_inc(sem("before"), 1)
                                if s % SG == 2:
                                    pe.wait_ge(sem("looked_up"), i * 2 + b + 1)
                                    for j in range(SG):
                                        last = t.matmul(ps_r[:, 0:j + 1, :], identb[:], four(OK[:, b, j, :], j + 1),
                                                        start=False, stop=True, skip_group_check=True)
                                    last.then_inc(sem("counted"), 1)
                            if c1:
                                n, i, s = c1
                                pe.wait_ge(sem("aT_sb"), upto(n))
                                pe.wait_ge(sem("silu"), upto(n - 2))
                                for h in range(DH):
                                    last = t.matmul(ps_z[s % 2][:, h, :], W1[:, h * P:(h + 1) * P], aT[:, s % 2, :], start=True, stop=True)
                                last.then_inc(sem("z"), 1)
                            if c3:
                                n, i, s = c3
                                pe.wait_ge(sem("silu"), upto(n))
                                pe.wait_ge(sem("gate"), upto(n - 2))
                                for h in range(DH):
                                    t.matmul(ps_g[s % 2][:], silu[:, s % 4, h * P:(h + 1) * P], W2[:, h, :], start=(h == 0), stop=False)
                                t.matmul(ps_g[s % 2][:], onesb[:], b2b[:], start=False, stop=True).then_inc(sem("g"), 1)

                    @block.vector
                    def _(dve):
                        v = nc.vector
                        dve.sem_inc(sem("counted"), 2)
                        credit(dve, "silu")
                        for c0, c3 in walk(nc.vector, NG // 2, 0, 3, width=SW):
                            if c0:
                                n, i, s = c0
                                b = s // SG
                                g = i * 2 + b
                                cols = ds(g * SG, SG)
                                if s % SG == 0:
                                    dve.wait_ge(sem("counted"), g + 1)
                                    one_hot_keys(g, b).then_inc(sem("hot"), 1)
                                if s % SG == 1:
                                    dve.wait_ge(sem("hot"), g + 1)
                                    dve.wait_ge(sem("before"), g + 1)
                                    v.tensor_tensor(prod[:, b, :, :], ps_r[:], OK[:, b, :, :], ALU.mult).then_inc(sem("looked_up"), 1)
                                if s % SG == 2:
                                    dve.wait_ge(sem("looked_up"), g + 1)
                                    v.tensor_reduce(posf[:, b, 0, :], prod[:, b, :, 0:KD], AX.X, ALU.add)
                                    v.tensor_reduce(posf[:, b, 1, :], prod[:, b, :, KD:K], AX.X, ALU.add).then_inc(sem("summed"), 1)
                                if s % SG == 3:
                                    dve.wait_ge(sem("summed"), g + 1)
                                    if not isinstance(i, int):
                                        for j in range(SG):
                                            dve.wait_ge(sem(f"sw_rec{b * SG + j}"), i * OUTS)
                                    v.tensor_tensor(pos[:, b, :], posf[:, b, 0, :], trash1[:, cols], ALU.add)
                                    v.tensor_tensor(place2[:, cols], posf[:, b, 1, :], trash2[:, cols], ALU.add)
                                    v.tensor_copy(rec[:, b, :, WMETA:WMETA + NMETA],
                                                  m1[:, :, cols].rearrange("p f c -> p c f")).then_inc(sem("placed"), 1)
                            if c3:
                                n, i, s = c3
                                dve.wait_ge(sem("sig"), upto(n))
                                dve.wait_ge(sem("g"), upto(n - 4))
                                v.tensor_tensor(silu[:, s % 4, :], ps_z[s % 2][:].rearrange("p h e -> p (h e)"), sig[:, s % 2, :],
                                                ALU.mult).then_inc(sem("silu"), 1)

                    @block.gpsimd
                    def _(pool):
                        pool.wait_ge(sem("emptied"), 16 * (1 + NC2 // EMPTY2 + KD))
                        with nc.gpsimd.Fori(0, NG // 2) as i:
                            for b in range(2):
                                g = i * 2 + b
                                for j in range(SG):
                                    waits = [(sem("gate"), upto(g * SG + j))]
                                    if j == 0:
                                        waits += [(sem("placed"), g + 1), (sem("a32"), upto(g))]
                                    wait_ahead(pool, *waits)
                                    pool.indirect_dma_start(
                                        rec_d, bass.IndirectOffsetOnAxis(ap=pos[:, b, j:j + 1], axis=0),
                                        rec[:, b, j, :], None).then_inc(sem(f"sw_rec{b * SG + j}"), 16)
                        for b in range(SW):
                            pool.wait_ge(sem(f"sw_rec{b}"), OUTS * (NG // 2))
                pctx.close()
                clear_semaphores()

        def scatter_by_source(pool, columns):
            width = G2 * GROUPS2
            first, last = columns[0] // width, columns[1] // width

            def turn(i, number):
                for g in range(GROUPS2):
                    if not isinstance(i, int):
                        wait_ahead(pool, (sem(f"sw_r{g}"), i * G2 * 16))
                    cols = ds(i * width + g * G2, G2)
                    nc.gpsimd.tensor_copy(now2[:, g, :, :], rows2[:, cols, :])
                    nc.gpsimd.tensor_copy(to2[:, g, :], place2[:, cols]).then_inc(sem("laid"), 1)
                    wait_ahead(pool, (sem("laid"), number * GROUPS2 + g + 1))
                    for j in range(G2):
                        pool.indirect_dma_start(rec2_d, bass.IndirectOffsetOnAxis(ap=to2[:, g, j:j + 1], axis=0),
                                                now2[:, g, j, :], None).then_inc(sem(f"sw_r{g}"), 16)
            if first == 0:
                turn(0, 0)
            with nc.gpsimd.Fori(max(first, 1), last) as i:
                turn(i, i - first)
            for g in range(GROUPS2):
                pool.wait_ge(sem(f"sw_r{g}"), last * G2 * 16)

        W_in = arena[:, 0:R8 * DH * D].rearrange("p (r h d) -> p r h d", r=R8, h=DH)
        meta2_at = T * (D + NH)
        meta2 = arena[:, meta2_at:meta2_at + NC2 * REC2].rearrange("p (n w) -> p n w", n=NC2)

        def normalize(keep=False, load_meta=False, early=()):
            ctx = ExitStack()
            with ctx:
                stats = sb(ctx, "stats", [P, T, 6])
                mean, var, rstd, nmr, t0 = (sb(ctx, n, [P, T]) for n in ("mean", "var", "rstd", "nmr", "t0"))
                hs = sb(ctx, "hs", [P, TG, D])
                ps_t = [ps(ctx, f"ps_t{b}", [P, DH, P]) for b in range(TG)]
                with nc.Block() as block:
                    @block.vector
                    def _(dve):
                        v, step = nc.vector, Chain(dve, sem("chain"))
                        with nc.vector.Fori(0, T) as t:
                            v.bn_stats(stats[:, ds(t), :], X[:, ds(t), :]).then_inc(sem("stats"), 1)
                        dve.wait_ge(sem("stats"), T)
                        m0, m1, s0, s1 = (stats[:, :, k] for k in (1, 4, 2, 5))
                        v.tensor_tensor(mean[:], m0, m1, ALU.add)
                        v.tensor_tensor(t0[:], m0, m1, ALU.subtract)
                        step(v.tensor_tensor(var[:], s0, s1, ALU.add))
                        v.tensor_scalar(mean[:], mean[:], 0.5, None, ALU.mult)
                        step(v.tensor_tensor(t0[:], t0[:], t0[:], ALU.mult))
                        step(v.tensor_scalar(t0[:], t0[:], 0.25, EPS, ALU.mult, ALU.add))
                        v.scalar_tensor_tensor(var[:], var[:], 1.0 / D, t0[:], ALU.mult, ALU.add).then_inc(sem("var"), 1)
                        dve.wait_ge(sem("root"), 1)
                        step(v.reciprocal(rstd[:], rstd[:]))
                        step(v.tensor_tensor(t0[:], rstd[:], rstd[:], ALU.mult))
                        step(v.tensor_tensor(t0[:], t0[:], var[:], ALU.mult))
                        step(v.tensor_scalar(t0[:], t0[:], -0.5, 1.5, ALU.mult, ALU.add))
                        step(v.tensor_tensor(rstd[:], rstd[:], t0[:], ALU.mult))
                        v.scalar_tensor_tensor(nmr[:], mean[:], -1.0, rstd[:], ALU.mult, ALU.mult).then_inc(sem("norm"), 1)
                        credit(dve, "hT_sb", "kept")
                        for c0, c1 in walk(nc.vector, T // TG, 0, 1, width=TG):
                            if c0 and keep:
                                t, i, s = c0
                                dve.wait_ge(sem("h"), upto(t))
                                v.tensor_tensor(X[:, ds(t), :], X[:, ds(t), :], hs[:, s:s + 1, :], ALU.add).then_inc(sem("kept"), 1)
                            if c1:
                                t, i, s = c1
                                dve.wait_ge(sem("turned"), upto(t))
                                v.tensor_copy(hT[:, ds(t), :, :], ps_t[s][:].unsqueeze(1)).then_inc(sem("hT_sb"), 1)

                    @block.scalar
                    def _(act):
                        act.wait_ge(sem("var"), 1)
                        nc.scalar.activation(rstd[:], var[:], ACT.Sqrt).then_inc(sem("root"), 1)
                        act.wait_ge(sem("norm"), 1)
                        credit(act, "h")
                        for (c0,) in walk(nc.scalar, T // TG, 0, width=TG):
                            if not c0:
                                continue
                            t, i, s = c0
                            act.wait_ge(sem("turned"), upto(t - TG))
                            if keep:
                                act.wait_ge(sem("kept"), upto(t - TG))
                            if not isinstance(i, int):
                                act.wait_ge(sem(f"h_out{s}"), i * 16)
                            nc.scalar.activation(hs[:, s:s + 1, :], X[:, ds(t), :], ACT.Relu, bias=nmr[:, ds(t)],
                                                 scale=rstd[:, ds(t)]).then_inc(sem("h"), 1)

                    @block.tensor
                    def _(pe):
                        credit(pe, "turned")
                        for (c0,) in walk(nc.tensor, T // TG, 0, width=TG):
                            if not c0:
                                continue
                            t, i, s = c0
                            pe.wait_ge(sem("h"), upto(t))
                            pe.wait_ge(sem("hT_sb"), upto(t - TG))
                            nc.tensor.transpose(ps_t[s][:, 0, :], hs[:, s, 0:P], ident[:])
                            nc.tensor.transpose(ps_t[s][:, 1, :], hs[:, s, P:D], ident[:]).then_inc(sem("turned"), 1)

                    @block.sync
                    def _(sp):
                        for to, of in early:
                            sp.dma_start(to, of).then_inc(sem("early_in"), 16)
                        if load_meta:
                            sp.dma_start(meta[:], rec_d[0:NC1 * P, WMETA:WMETA + NMETA].rearrange(
                                "(j p) w -> p j w", p=P)).then_inc(sem("meta_in"), 16)
                        with nc.sync.Fori(0, T // TG) as i:
                            for s in range(TG):
                                t = i * TG + s
                                sp.wait_ge(sem("h"), upto(t))
                                sp.dma_start(h_d[ds(t * P, P), :], hs[:, s, :]).then_inc(sem(f"h_out{s}"), 16)
                        for s in range(TG):
                            sp.wait_ge(sem(f"h_out{s}"), 16 * (T // TG))
                        if load_meta:
                            sp.wait_ge(sem("meta_in"), 16)
                        if early:
                            sp.wait_ge(sem("early_in"), 16 * len(early))

                    if keep:
                        @block.gpsimd
                        def _(pool):
                            scatter_by_source(pool, (240, 272))

                    if load_meta:
                        @block.gpsimd
                        def _(pool):
                            pool.wait_ge(sem("meta_in"), 16)
                            nc.gpsimd.tensor_copy(idx[:, 0, :], meta[:, :, 1])
                            nc.gpsimd.tensor_copy(idx[:, 1, :], meta[:, :, 2]).then_inc(sem("indices"), 1)
                            pool.wait_ge(sem("indices"), 1)
                clear_semaphores()

        def one_hot_distance(act, chunk, column, dist):
            n, _, s = chunk
            act.wait_ge(sem("hot"), upto(n - 2))
            nc.scalar.activation(dist[:, s % 2, :], iota[:, 0:P], ACT.Abs, bias=column, scale=-1.0).then_inc(sem("dist"), 1)

        def one_hot_row(act, chunk, dist, to):
            n, _, s = chunk
            act.wait_ge(sem("dist"), upto(n))
            nc.scalar.activation(to, dist[:, s % 2, :], ACT.Relu, bias=ones[:, 0:1], scale=-1.0).then_inc(sem("hot"), 1)

        def load_indices(sp, which, i, q, ixs, free, width=U, part=QU):
            sp.wait_ge(sem(free), i * width + (q + 1) * part - width + CREDIT)
            sp.dma_start(ixs[:, q * part:(q + 1) * part],
                         idx[:, which, ds(i * width + q * part, part)]).then_inc(sem(f"ix_in{q}"), 16)

        def gather_rows(pool, turns, table, ixs, G, free, width=U, part=QU):
            with nc.gpsimd.Fori(0, turns) as i:
                for s in range(width):
                    waits = [(sem(free), i * width + s + 1 - width + CREDIT)]
                    if s % part == 0:
                        waits.append((sem(f"ix_in{s // part}"), (i + 1) * 16))
                    wait_ahead(pool, *waits)
                    pool.indirect_dma_start(G[:, s, :], None, table, bass.IndirectOffsetOnAxis(
                        ap=ixs[:, s:s + 1], axis=0)).then_inc(sem(f"sw_g{s}"), 16)

        acc0 = arena[:].rearrange("p (b c) -> p b c", b=KD)

        def rgcn():
            ctx = ExitStack()
            with ctx:
                nnw_in = sb(ctx, "nnw_in", [P, DH, A32])
                nnw = sb(ctx, "nnw", [P, D])
                W = sb(ctx, "W", [P, R3, DH, D])
                root = sb(ctx, "root", [P, DH, D])
                bias = sb(ctx, "bias", [P, D])
                attT = sb(ctx, "attT", [P, 2, HU, P])

                with ExitStack() as pctx:
                    ps_w = ps(pctx, "ps_w", [A32, D])
                    with nc.Block() as block:
                        @block.vector
                        def _(dve):
                            step = Chain(dve, sem("chain_v"))
                            nc.vector.memset(nnw[:], 0.0).then_inc(sem("w_clear"), 1)
                            step(nc.vector.memset(attT[:], 0.0))
                            step(nc.vector.memset(attT[A32:A32 + 1, :, :, :], 1.0))

                        @block.sync
                        def _(sp):
                            sp.dma_start(nnw_in[:], L0_gnn_nn_w.rearrange("(h p) a -> p h a", p=P)).then_inc(sem("w_in"), 16)
                            sp.wait_ge(sem("w_clear"), 1)
                            sp.dma_start(nnw[A32:A32 + 1, :], L0_gnn_nn_b.rearrange("(a d) -> a d", a=1)).then_inc(sem("w_in"), 16)

                        @block.tensor
                        def _(pe):
                            pe.wait_ge(sem("w_in"), 32)
                            nc.tensor.transpose(ps_w[:, 0:P], nnw_in[:, 0, :], ident[:])
                            nc.tensor.transpose(ps_w[:, P:D], nnw_in[:, 1, :], ident[:]).then_inc(sem("turned"), 1)

                        @block.scalar
                        def _(act):
                            act.wait_ge(sem("turned"), 1)
                            act.wait_ge(sem("w_in"), 32)
                            nc.scalar.copy(nnw[0:A32, :], ps_w[:]).then_inc(sem("chain"), 1)
                            act.wait_ge(sem("chain"), 1)
                    clear_semaphores()

                def layer(l):
                    gathered = l * TURNS1
                    pctx = ExitStack()
                    with pctx:
                        att = sb(pctx, "att", [P, 2, HU, A32]) if l == 0 else None
                        ixs = sb(pctx, "ixs", [P, U], I32)
                        G = sb(pctx, "G", [P, U, D])
                        prod = sb(pctx, "prodm", [P, 2, D]) if l > 0 else None
                        msg = sb(pctx, "msg", [P, RING, D])
                        hot = sb(pctx, "hotm", [P, U, P])
                        dist = sb(pctx, "dist", [P, 2, P])
                        ps_t = [ps(pctx, f"ps_t{b}", [A32, P]) for b in range(2)]
                        ps_e = [ps(pctx, f"ps_e{b}", [P, D]) for b in range(BANKS)]
                        ps_a = [ps(pctx, f"ps_a{b}", [P, DH, P]) for b in range(BANKS)]
                        with nc.Block() as block:
                            @block.sync
                            def _(sp):
                                sp.dma_start(W[:], L0_gnn_W[l].rearrange("r (h p) d -> p r h d", p=P)).then_inc(sem("w_in"), 16)
                                sp.dma_start(root[:], L0_gnn_root[l].rearrange("(h p) d -> p h d", p=P)).then_inc(sem("w_in"), 16)
                                sp.dma_start(bias[:], L0_gnn_bias[l:l + 1, :].to_broadcast([P, D])).then_inc(sem("w_in"), 16)
                                with nc.sync.Fori(0, TURNS1) as i:
                                    for h in range(2):
                                        chunks = i * U + h * HU
                                        if l == 0:
                                            sp.wait_ge(sem("attT"), upto(chunks + HU - 1 - U))
                                            sp.dma_start(att[:, h, :, :], rec_d[ds(chunks * P, HU * P), WA32:REC].rearrange(
                                                "(j p) w -> p j w", p=P)).then_inc(sem(f"att_in{h}"), 16)
                                        else:
                                            sp.wait_ge(sem("ew"), upto(chunks + HU - 1 - U))
                                            sp.dma_start(attT[0:A32, h, :, :], attT_d[:, ds(chunks, HU), :]).then_inc(sem(f"att_in{h}"), 16)
                                        for q in range(h * (HU // QU), (h + 1) * (HU // QU)):
                                            load_indices(sp, 0, i, q, ixs, "prod")
                                sp.wait_ge(sem("w_in"), 48)

                            @block.gpsimd
                            def _(pool):
                                gather_rows(pool, TURNS1, h_d, ixs, G, "prod")

                            @block.tensor
                            def _(pe):
                                t = nc.tensor
                                credit(pe, "attT", "ew", "agg")
                                for c0, c1, c7 in walk(nc.tensor, TURNS1, 0, 1, 7):
                                    if c0 and l == 0:
                                        n, i, s = c0
                                        if s % HU == 0:
                                            pe.wait_ge(sem(f"att_in{s // HU}"), (i + 1) * 16)
                                        pe.wait_ge(sem("attT_sb"), upto(n - 2))
                                        t.transpose(ps_t[s % 2][:], att[:, s // HU, s % HU, :], ident[:]).then_inc(sem("attT"), 1)
                                    if c1:
                                        n, i, s = c1
                                        if l == 0:
                                            pe.wait_ge(sem("attT_sb"), upto(n))
                                        elif s % HU == 0:
                                            pe.wait_ge(sem(f"att_in{s // HU}"), (i + 1) * 16)
                                        pe.wait_ge(sem("prod"), upto(n - BANKS))
                                        t.matmul(ps_e[s % BANKS][:], attT[:, s // HU, s % HU, :], nnw[:], start=True, stop=True).then_inc(sem("ew"), 1)
                                    if c7:
                                        n, i, s = c7
                                        pe.wait_ge(sem("prod" if l == 0 else "msg"), upto(n))
                                        pe.wait_ge(sem("hot"), upto(n))
                                        pe.wait_ge(sem("acc"), upto(n - BANKS))
                                        for h in range(DH):
                                            last = t.matmul(ps_a[s % BANKS][:, h, :], msg[:, s % RING, h * P:(h + 1) * P], hot[:, s, :],
                                                            start=True, stop=True)
                                        last.then_inc(sem("agg"), 1)

                            @block.scalar
                            def _(act):
                                credit(act, "attT_sb", "dist", "hot", *(["msg"] if l > 0 else []))
                                for c0, c1, c3 in walk(nc.scalar, TURNS1, 0, 1, 3):
                                    if c0:
                                        n, i, s = c0
                                        if l == 0:
                                            act.wait_ge(sem("attT"), upto(n))
                                            act.wait_ge(sem("ew"), upto(n - U))
                                            if s % HU == 0 and not isinstance(i, int):
                                                act.wait_ge(sem(f"att_out{s // HU}"), i * 16)
                                            nc.scalar.copy(attT[0:A32, s // HU, s % HU, :], ps_t[s % 2][:]).then_inc(sem("attT_sb"), 1)
                                        one_hot_distance(act, c0, meta[:, ds(n), 0], dist)
                                    if c1:
                                        n, i, s = c1
                                        act.wait_ge(sem("agg"), upto(n - U))
                                        one_hot_row(act, c1, dist, hot[:, s, :])
                                        if l == 0 and s % HU == HU - 1:
                                            wait_ahead(act, (sem("attT_sb"), upto(n)))
                                            nc.scalar.dma_start(attT_d[:, ds(n - (HU - 1), HU), :], attT[0:A32, s // HU, :, :]).then_inc(
                                                sem(f"att_out{s // HU}"), 16)
                                    if c3 and l > 0:
                                        n, i, s = c3
                                        act.wait_ge(sem("prod"), upto(n))
                                        act.wait_ge(sem("agg"), upto(n - RING))
                                        nc.scalar.activation(msg[:, s % RING, :], prod[:, s % 2, :], ACT.Relu).then_inc(sem("msg"), 1)
                                if l == 0:
                                    for h in range(2):
                                        act.wait_ge(sem(f"att_out{h}"), 16 * TURNS1)

                            @block.vector
                            def _(dve):
                                v = nc.vector
                                credit(dve, "prod", "acc")
                                v.memset(arena[:], 0.0).then_inc(sem("zeroed"), 1)
                                dve.wait_ge(sem("zeroed"), 1)
                                bucket = Buckets(nc, mybir.EngineType.DVE, bmap[0:1, 0, :], KD - 1, 8)
                                for c2, c8 in walk(nc.vector, TURNS1, 2, 8):
                                    if c2:
                                        n, i, s = c2
                                        dve.wait_ge(sem(f"sw_g{s}"), (gathered + i + 1) * 16)
                                        dve.wait_ge(sem("ew"), upto(n))
                                        if l == 0:
                                            dve.wait_ge(sem("agg"), upto(n - RING))
                                            v.scalar_tensor_tensor(msg[:, s % RING, :], ps_e[s % BANKS][:], 0.0, G[:, s, :],
                                                                   ALU.max, ALU.mult).then_inc(sem("prod"), 1)
                                        else:
                                            dve.wait_ge(sem("msg"), upto(n - 2))
                                            v.tensor_tensor(prod[:, s % 2, :], G[:, s, :], ps_e[s % BANKS][:], ALU.mult).then_inc(sem("prod"), 1)
                                    if c8:
                                        n, i, s = c8
                                        b = bucket(c8)
                                        dve.wait_ge(sem("agg"), upto(n))
                                        dve.wait_ge(sem("acc"), upto(n - 1))
                                        to = acc0[:, ds(b), :]
                                        v.tensor_tensor(to, ps_a[s % BANKS][:].rearrange("p h n -> p (h n)").unsqueeze(1), to, ALU.add).then_inc(sem("acc"), 1)
                        clear_semaphores()

                    with ExitStack() as pctx:
                        cur = sb(pctx, "cur", [P, 2, (R3 + 1) * D])
                        hn = sb(pctx, "hn", [P, TG, D])
                        ps_o = [ps(pctx, f"ps_o{b}", [P, R3 + 1, D]) for b in range(2)]
                        ps_t = [ps(pctx, f"ps_t{b}", [P, DH, P]) for b in range(2)]
                        final = l == 2
                        PER = R3 + 1
                        with nc.Block() as block:
                            @block.gpsimd
                            def _(pool):
                                scatter_by_source(pool, (l * 80, (l + 1) * 80))

                            @block.scalar
                            def _(act):
                                credit(act, "cur", "hT_sb")
                                for c0, c2 in walk(nc.scalar, T // TG, 0, 2, width=TG):
                                    if c0:
                                        t, i, s = c0
                                        wait_ahead(act, (sem("outs"), (t - since(s) + 1 + CREDIT) * PER))
                                        nc.scalar.copy(cur[:, s % 2, 0:D], hT[:, ds(t), :, :].rearrange("p t h n -> p (t h n)"))
                                        nc.scalar.copy(cur[:, s % 2, D:].rearrange("p (r c) -> p r c", r=R3),
                                                       acc0[:, ds(t * R3, R3), :]).then_inc(sem("cur"), 1)
                                    if c2 and not final:
                                        t, i, s = c2
                                        wait_ahead(act, (sem("turned"), upto(t)), (sem("cur"), upto(t)))
                                        nc.scalar.copy(hT[:, ds(t), :, :], ps_t[s % 2][:].unsqueeze(1)).then_inc(sem("hT_sb"), 1)

                            @block.tensor
                            def _(pe):
                                credit(pe, "turned")
                                pe.sem_inc(sem("outs"), CREDIT * PER)
                                for c0, c1 in walk(nc.tensor, T // TG, 0, 1, width=TG):
                                    if c0:
                                        t, i, s = c0
                                        pe.wait_ge(sem("cur"), upto(t))
                                        for r in range(PER):
                                            pe.wait_ge(sem("added"), (t - since(s) + CREDIT) * PER + (r | 1) + 1)
                                            for h in range(DH):
                                                w = root[:, h, :] if r == 0 else W[:, r - 1, h, :]
                                                last = nc.tensor.matmul(ps_o[s % 2][:, r, :], cur[:, s % 2, r * D + h * P:r * D + (h + 1) * P], w,
                                                                        start=(h == 0), stop=(h == DH - 1))
                                            last.then_inc(sem("outs"), 1)
                                    if c1 and not final:
                                        t, i, s = c1
                                        pe.wait_ge(sem("added"), (t + 1 + CREDIT) * PER)
                                        pe.wait_ge(sem("hT_sb"), upto(t - since(s)))
                                        nc.tensor.transpose(ps_t[s % 2][:, 0, :], hn[:, s, 0:P], ident[:])
                                        nc.tensor.transpose(ps_t[s % 2][:, 1, :], hn[:, s, P:D], ident[:]).then_inc(sem("turned"), 1)

                            @block.vector
                            def _(dve):
                                v = nc.vector
                                credit(dve, "x")
                                dve.sem_inc(sem("added"), CREDIT * PER)
                                for (c0,) in walk(nc.vector, T // TG, 0, width=TG):
                                    if not c0:
                                        continue
                                    t, i, s = c0
                                    done = (t + CREDIT) * PER
                                    if not final:
                                        dve.wait_ge(sem("turned"), upto(t - TG))
                                        if not isinstance(i, int):
                                            dve.wait_ge(sem(f"h_out{s}"), i * 16)
                                    else:
                                        dve.wait_ge(sem("x"), upto(t - TG))
                                    dve.wait_ge(sem("outs"), done + 2)
                                    v.tensor_tensor(hn[:, s, :], ps_o[s % 2][:, 0, :], bias[:], ALU.add).then_inc(sem("added"), 1)
                                    for r in range(R3):
                                        dve.wait_ge(sem("added"), done + 1 + r)
                                        dve.wait_ge(sem("outs"), done + ((r + 1) | 1) + 1)
                                        v.scalar_tensor_tensor(hn[:, s, :], ps_o[s % 2][:, r + 1, :], inv_cnt[:, ds(t * R3 + r)], hn[:, s, :],
                                                               ALU.mult, ALU.add).then_inc(sem("added"), 1)
                                    if final:
                                        dve.wait_ge(sem("added"), done + PER)
                                        v.tensor_tensor(X[:, ds(t), :], X[:, ds(t), :], hn[:, s:s + 1, :], ALU.add).then_inc(sem("x"), 1)

                            if not final:
                                @block.sync
                                def _(sp):
                                    with nc.sync.Fori(0, T // TG) as i:
                                        for s in range(TG):
                                            t = i * TG + s
                                            sp.wait_ge(sem("added"), (t + 1 + CREDIT) * PER)
                                            sp.dma_start(h_d[ds(t * P, P), :], hn[:, s, :]).then_inc(sem(f"h_out{s}"), 16)
                                    for s in range(TG):
                                        sp.wait_ge(sem(f"h_out{s}"), 16 * (T // TG))
                        clear_semaphores()

                for l in range(3):
                    layer(l)

        def gated():
            gathered = 3 * TURNS1
            acc1 = arena[:, 0:T * D].rearrange("p (t h n) -> p t h n", t=T, h=DH)
            ctx = ExitStack()
            with ctx:
                U1 = sb(ctx, "U1", [P, 2 * DH, D])
                U2 = sb(ctx, "U2", [P, DH, D])
                c1 = sb(ctx, "c1", [P, DH])
                c2 = sb(ctx, "c2", [P, D])
                ixs = sb(ctx, "ixs", [P, U], I32)
                gate = sb(ctx, "gate", [P, U, D])
                G = sb(ctx, "G", [P, U, D])
                msg = sb(ctx, "msg", [P, RING, D])
                hot = sb(ctx, "hotm", [P, RING, P])
                dist = sb(ctx, "dist", [P, 2, P])
                sig = arena[:, T * D:(T + TG) * D].rearrange("p (s h n) -> p s h n", s=TG, h=DH)
                silu = arena[:, (T + TG) * D:(T + 2 * TG) * D].rearrange("p (s h n) -> p s h n", s=TG, h=DH)
                upd = sb(ctx, "upd", [P, 2, D])
                with ExitStack() as pctx:
                    ps_a = [ps(pctx, f"ps_a{b}", [P, DH, P]) for b in range(BANKS)]
                    with nc.Block() as block:
                        @block.sync
                        def _(sp):
                            sp.dma_start(U1[:], L1_gnn_U1.rearrange("(h p) d -> p h d", p=P)).then_inc(sem("w_in"), 16)
                            sp.dma_start(U2[:], L1_gnn_U2.rearrange("(h p) d -> p h d", p=P)).then_inc(sem("w_in"), 16)
                            for h in range(DH):
                                sp.dma_start(c1[:, h:h + 1], L1_gnn_c1[h * P:(h + 1) * P].rearrange("(p a) -> p a", a=1)).then_inc(sem("w_in"), 16)
                            sp.dma_start(c2[:], L1_gnn_c2.rearrange("(a d) -> a d", a=1).to_broadcast([P, D])).then_inc(sem("w_in"), 16)
                            with nc.sync.Fori(0, TURNS1) as i:
                                for q in range(U // QU):
                                    chunks = i * U + q * QU
                                    load_indices(sp, 0, i, q, ixs, "msg")
                                    sp.dma_start(gate[:, q * QU:(q + 1) * QU, :], rec_d[ds(chunks * P, QU * P), 0:D].rearrange(
                                        "(j p) w -> p j w", p=P)).then_inc(sem(f"gate_in{q}"), 16)
                            sp.wait_ge(sem("w_in"), 80)

                        @block.gpsimd
                        def _(pool):
                            gather_rows(pool, TURNS1, h_d, ixs, G, "msg")

                        @block.tensor
                        def _(pe):
                            credit(pe, "agg")
                            for (c3,) in walk(nc.tensor, TURNS1, 3):
                                if c3:
                                    n, i, s = c3
                                    pe.wait_ge(sem("msg"), upto(n))
                                    pe.wait_ge(sem("hot"), upto(n))
                                    pe.wait_ge(sem("acc"), upto(n - BANKS))
                                    for h in range(DH):
                                        last = nc.tensor.matmul(ps_a[s % BANKS][:, h, :], msg[:, s % RING, h * P:(h + 1) * P],
                                                                hot[:, s % RING, :], start=True, stop=True)
                                    last.then_inc(sem("agg"), 1)

                        @block.scalar
                        def _(act):
                            credit(act, "dist", "hot")
                            for c0, c1 in walk(nc.scalar, TURNS1, 0, 1):
                                if c0:
                                    one_hot_distance(act, c0, meta[:, ds(c0[0]), 0], dist)
                                if c1:
                                    n, i, s = c1
                                    act.wait_ge(sem("agg"), upto(n - RING))
                                    one_hot_row(act, c1, dist, hot[:, s % RING, :])

                        @block.vector
                        def _(dve):
                            v = nc.vector
                            credit(dve, "msg", "acc")
                            v.memset(acc1, 0.0).then_inc(sem("zeroed"), 1)
                            dve.wait_ge(sem("zeroed"), 1)
                            bucket = Buckets(nc, mybir.EngineType.DVE, bmap[0:1, 1, :], T - 1, 4)
                            for c0, c4 in walk(nc.vector, TURNS1, 0, 4):
                                if c0:
                                    n, i, s = c0
                                    dve.wait_ge(sem("agg"), upto(n - RING))
                                    dve.wait_ge(sem(f"sw_g{s}"), (gathered + i + 1) * 16)
                                    if s % QU == 0:
                                        dve.wait_ge(sem(f"gate_in{s // QU}"), (i + 1) * 16)
                                    v.tensor_tensor(msg[:, s % RING, :], G[:, s, :], gate[:, s, :],
                                                    ALU.mult).then_inc(sem("msg"), 1)
                                if c4:
                                    n, i, s = c4
                                    b = bucket(c4)
                                    dve.wait_ge(sem("agg"), upto(n))
                                    dve.wait_ge(sem("acc"), upto(n - 1))
                                    to = acc1[:, ds(b), :, :]
                                    v.tensor_tensor(to, ps_a[s % BANKS][:].unsqueeze(1), to, ALU.add).then_inc(sem("acc"), 1)
                    clear_semaphores()

                with ExitStack() as pctx:
                    ps_z = [ps(pctx, f"ps_z{b}", [P, DH, P]) for b in range(5)]
                    ps_o = [ps(pctx, f"ps_o{b}", [P, D]) for b in range(3)]
                    with nc.Block() as block:
                        @block.gpsimd
                        def _(pool):
                            scatter_by_source(pool, (272, 328))

                        @block.tensor
                        def _(pe):
                            t_ = nc.tensor
                            credit(pe, "z", "o")
                            for c0, c1_ in walk(nc.tensor, T // 5, 0, 2, width=5):
                                if c0:
                                    t, i, s = c0
                                    pe.wait_ge(sem("silu"), upto(t - 5))
                                    for h in range(DH):
                                        for k in range(2 * DH):
                                            of = hT if k < DH else acc1
                                            last = t_.matmul(ps_z[s][:, h, :], U1[:, k, h * P:(h + 1) * P],
                                                             of[:, ds(t), k % DH, :].rearrange("p t n -> p (t n)"),
                                                             start=(k == 0), stop=(k == 2 * DH - 1))
                                    last.then_inc(sem("z"), 1)
                                if c1_:
                                    t, i, s = c1_
                                    pe.wait_ge(sem("silu"), upto(t))
                                    pe.wait_ge(sem("x"), upto(t - 1))
                                    for h in range(DH):
                                        last = t_.matmul(ps_o[s % 2][:], silu[:, s, h, :], U2[:, h, :], start=(h == 0), stop=(h == DH - 1))
                                    last.then_inc(sem("o"), 1)

                        @block.scalar
                        def _(act):
                            credit(act, "sig")
                            for (c0,) in walk(nc.scalar, T // 5, 0, width=5):
                                if c0:
                                    t, i, s = c0
                                    act.wait_ge(sem("z"), upto(t))
                                    act.wait_ge(sem("silu"), upto(t - 5))
                                    for h in range(DH):
                                        last = nc.scalar.activation(sig[:, s, h, :], ps_z[s][:, h, :], ACT.Sigmoid, bias=c1[:, h:h + 1])
                                    last.then_inc(sem("sig"), 1)

                        @block.vector
                        def _(dve):
                            v = nc.vector
                            credit(dve, "silu", "x")
                            dve.sem_inc(sem("upd"), CREDIT)
                            for c0, c1_ in walk(nc.vector, T // 5, 0, 2, width=5):
                                if c0:
                                    t, i, s = c0
                                    dve.wait_ge(sem("sig"), upto(t))
                                    dve.wait_ge(sem("o"), upto(t - 5))
                                    for h in range(DH):
                                        last = v.scalar_tensor_tensor(silu[:, s, h, :], ps_z[s][:, h, :], c1[:, h:h + 1],
                                                                      sig[:, s, h, :], ALU.add, ALU.mult)
                                    last.then_inc(sem("silu"), 1)
                                if c1_:
                                    t, i, s = c1_
                                    dve.wait_ge(sem("o"), upto(t))
                                    dve.wait_ge(sem("x"), upto(t - 1))
                                    v.tensor_tensor(upd[:, 0, :], ps_o[s % 2][:], c2[:], ALU.add).then_inc(sem("upd"), 1)
                                    dve.wait_ge(sem("upd"), upto(t))
                                    v.tensor_tensor(X[:, ds(t), :], X[:, ds(t), :], upd[:, 0:1, :], ALU.add).then_inc(sem("x"), 1)
                    clear_semaphores()

        def relational_attention():
            WC = D + 2 * NH
            ctx = ExitStack()
            with ctx:
                ixs = sb(ctx, "ixs", [P, U], I32)
                adT = sb(ctx, "adT", [P, T, NH * R8])
                LG = sb(ctx, "LG", [P, NC1, NH])
                with ExitStack() as pctx:
                    scratch = arena[:, R8 * DH * D:2 * R8 * DH * D]
                    WT = sb(pctx, "WT", [P, DH, R8, WC])
                    a_row = sb(pctx, "a_row", [P, 2, D])
                    cur = sb(pctx, "cur", [P, 2, D])
                    stage = sb(pctx, "stage", [P, 2, R8, WC])
                    ps_b = [ps(pctx, f"ps_b{b}", [P, 512]) for b in range(8)]
                    with nc.Block() as block:
                        @block.sync
                        def _(sp):
                            for m, a in enumerate((L2_gnn_a_src, L2_gnn_a_dst)):
                                sp.dma_start(a_row[:, m, :], a.rearrange("(a h) d -> a (h d)", a=1).to_broadcast([P, D])).then_inc(sem("w_in"), 16)

                        @block.tensor
                        def _(pe):
                            for r in range(R8):
                                for k in range(DH):
                                    for h in range(DH):
                                        last = nc.tensor.transpose(ps_b[r][:, k * D + h * P:k * D + (h + 1) * P],
                                                                   W_in[:, r, h, k * P:(k + 1) * P], ident[:])
                                last.then_inc(sem("turned"), 1)

                        @block.vector
                        def _(dve):
                            v, step = nc.vector, Chain(dve, sem("chain"))
                            dve.wait_ge(sem("w_in"), 32)
                            for r in range(R8):
                                dve.wait_ge(sem("turned"), r + 1)
                                last = v.tensor_copy(WT[:, :, r, 0:D], ps_b[r][:].rearrange("p (k d) -> p k d", k=DH))
                            step(last)
                            rows = WT[:].rearrange("p k r c -> p (k r) c")
                            for m in range(2):
                                step(v.tensor_tensor(scratch.rearrange("p (k d) -> p k d", d=D), rows[:, :, 0:D],
                                                     a_row[:, m:m + 1, :].to_broadcast([P, DH * R8, D]), ALU.mult))
                                step(v.tensor_reduce(rows[:, :, D + m * NH:D + (m + 1) * NH],
                                                     scratch.rearrange("p (k h d) -> p k h d", h=NH, d=HD), AX.X, ALU.add))
                    clear_semaphores()
                    with nc.Block() as block:
                        @block.gpsimd
                        def _(pool):
                            scatter_by_source(pool, (328, EC))

                        @block.tensor
                        def _(pe):
                            pe.sem_inc(sem("rows"), CREDIT * R8)
                            for t, b in tiles(nc.tensor):
                                pe.wait_ge(sem("cur"), upto(t))
                                for r in range(R8):
                                    pe.wait_ge(sem(f"copied{r % 2}"), (t + CREDIT - 1) * 4 + r // 2 + 1)
                                    for h in range(DH):
                                        last = nc.tensor.matmul(ps_b[r][:, 0:WC], cur[:, b, h * P:(h + 1) * P], WT[:, h, r, :],
                                                                start=(h == 0), stop=(h == DH - 1))
                                    last.then_inc(sem("rows"), 1)

                        @block.scalar
                        def _(act):
                            credit(act, "cur")
                            act.sem_inc(sem("copied0"), CREDIT * 4)
                            for t, b in tiles(nc.scalar):
                                wait_ahead(act, (sem("rows"), (t + CREDIT - 1) * R8))
                                nc.scalar.copy(cur[:, b, :], hT[:, ds(t), :, :].rearrange("p t h n -> p (t h n)")).then_inc(sem("cur"), 1)
                                act.wait_ge(sem("stored"), upto(t - 2))
                                for r in range(0, R8, 2):
                                    act.wait_ge(sem("rows"), (t + CREDIT) * R8 + r + 1)
                                    nc.scalar.copy(stage[:, b, r, :], ps_b[r][:, 0:WC]).then_inc(sem("copied0"), 1)

                        @block.vector
                        def _(dve):
                            v = nc.vector
                            dve.sem_inc(sem("copied1"), CREDIT * 4)
                            credit(dve, "ad")
                            for t, b in tiles(nc.vector):
                                dve.wait_ge(sem("stored"), upto(t - 2))
                                for r in range(1, R8, 2):
                                    dve.wait_ge(sem("rows"), (t + CREDIT) * R8 + r + 1)
                                    v.tensor_copy(stage[:, b, r, :], ps_b[r][:, 0:WC]).then_inc(sem("copied1"), 1)
                                dve.wait_ge(sem("copied0"), (t + CREDIT + 1) * 4)
                                dve.wait_ge(sem("copied1"), (t + CREDIT + 1) * 4)
                                v.tensor_copy(adT[:, ds(t), :].rearrange("p t (h r) -> p (t h) r", h=NH),
                                              stage[:, b, :, D + NH:WC].rearrange("p r h -> p h r")).then_inc(sem("ad"), 1)

                        @block.sync
                        def _(sp):
                            credit(sp, "stored")
                            for t, b in tiles(nc.sync):
                                sp.wait_ge(sem("ad"), upto(t))
                                sp.dma_start(rel_d.rearrange("(r n) w -> n r w", r=R8)[ds(t * P, P), :, :],
                                             stage[:, b, :, 0:D]).then_inc(sem("rel_out"), 16)
                                sp.dma_start(relatt_d.rearrange("(r n) w -> n r w", r=R8)[ds(t * P, P), :, :],
                                             stage[:, b, :, D:D + NH]).then_inc(sem("rel_out"), 16)
                                sp.wait_ge(sem("rel_out"), (t + 1) * 32)
                                sp.sem_inc(sem("stored"), 1)
                    clear_semaphores()

                with ExitStack() as pctx:
                    gathered = 4 * TURNS1
                    ga = sb(pctx, "ga", [P, U, NH])
                    hot = sb(pctx, "hotm", [P, RING, P])
                    hotT = sb(pctx, "hotT", [P, RING, P])
                    of_rel = sb(pctx, "of_rel", [P, HU, R8])
                    picked = sb(pctx, "picked", [P, HU, NH, R8])
                    summed = sb(pctx, "summed", [P, HU, NH])
                    ps_t = [ps(pctx, f"ps_t{b}", [P, P]) for b in range(2)]
                    ps_d = [ps(pctx, f"ps_d{b}", [P, HU, NH * R8]) for b in range(2)]
                    with nc.Block() as block:
                        @block.sync
                        def _(sp):
                            with nc.sync.Fori(0, TURNS1) as i:
                                for h in range(2):
                                    sp.wait_ge(sem("logits"), upto(i * 2 + h - 2))
                                    sp.dma_start(ixs[:, h * HU:(h + 1) * HU],
                                                 idx[:, 1, ds(i * U + h * HU, HU)]).then_inc(sem(f"ix_in{h}"), 16)

                        @block.gpsimd
                        def _(pool):
                            with nc.gpsimd.Fori(0, TURNS1) as i:
                                for s in range(U):
                                    if s % HU == 0:
                                        wait_ahead(pool, (sem("logits"), upto(i * 2 + s // HU - 2)), (sem(f"ix_in{s // HU}"), (i + 1) * 16))
                                    pool.indirect_dma_start(ga[:, s, :], None, relatt_d, bass.IndirectOffsetOnAxis(
                                        ap=ixs[:, s:s + 1], axis=0)).then_inc(sem(f"sw_g{s}"), 16)

                        @block.tensor
                        def _(pe):
                            credit(pe, "hotT", "ad_e")
                            bucket = Buckets(nc, mybir.EngineType.PE, bmap[0:1, 1, :], T - 1, 4, part=RING)
                            for c0, c4 in walk(nc.tensor, TURNS1, 0, 4):
                                if c0:
                                    n, i, s = c0
                                    pe.wait_ge(sem("hot"), upto(n))
                                    pe.wait_ge(sem("hotT_sb"), upto(n - 2))
                                    nc.tensor.transpose(ps_t[s % 2][:], hot[:, s % RING, :], ident[:]).then_inc(sem("hotT"), 1)
                                if c4:
                                    n, i, s = c4
                                    b = bucket(c4)
                                    pe.wait_ge(sem("hotT_sb"), upto(n))
                                    if s % HU == 0:
                                        pe.wait_ge(sem("logits"), upto(i * 2 + s // HU - 2))
                                    nc.tensor.matmul(ps_d[s // HU][:, s % HU, :], hotT[:, s % RING, :],
                                                     adT[:, ds(b), :].rearrange("p t c -> p (t c)"), start=True, stop=True).then_inc(sem("ad_e"), 1)

                        @block.scalar
                        def _(act):
                            credit(act, "hotT_sb")
                            for (c0,) in walk(nc.scalar, TURNS1, 0):
                                if c0:
                                    n, i, s = c0
                                    act.wait_ge(sem("hotT"), upto(n))
                                    act.wait_ge(sem("ad_e"), upto(n - RING))
                                    nc.scalar.copy(hotT[:, s % RING, :], ps_t[s % 2][:]).then_inc(sem("hotT_sb"), 1)

                        @block.vector
                        def _(dve):
                            v = nc.vector
                            credit(dve, "hot", "logits")
                            dve.sem_inc(sem("picked"), CREDIT * 3)
                            for c0, c5 in walk(nc.vector, TURNS1, 0, 5):
                                if c0:
                                    n, i, s = c0
                                    dve.wait_ge(sem("hotT"), upto(n - RING))
                                    v.tensor_scalar(hot[:, s % RING, :], iota[:, 0:P], meta[:, ds(n), 0], None, ALU.is_equal).then_inc(sem("hot"), 1)
                                if c5 and c5[2] % HU == HU - 1:
                                    n, i, s = c5
                                    half = i * 2 + s // HU
                                    chunks = ds(n - (HU - 1), HU)
                                    dve.wait_ge(sem("picked"), (half + CREDIT) * 3)
                                    v.tensor_tensor(of_rel[:], meta[:, chunks, 3].unsqueeze(2).to_broadcast([P, HU, R8]),
                                                    iota[:, 0:R8].unsqueeze(1).to_broadcast([P, HU, R8]), ALU.is_equal).then_inc(sem("picked"), 1)
                                    dve.wait_ge(sem("ad_e"), upto(n))
                                    dve.wait_ge(sem("picked"), (half + CREDIT) * 3 + 1)
                                    v.tensor_tensor(picked[:], ps_d[s // HU][:].rearrange("p j (h r) -> p j h r", h=NH),
                                                    of_rel[:].unsqueeze(2).to_broadcast([P, HU, NH, R8]), ALU.mult).then_inc(sem("picked"), 1)
                                    dve.wait_ge(sem("picked"), (half + CREDIT) * 3 + 2)
                                    v.tensor_reduce(summed[:], picked[:], AX.X, ALU.add).then_inc(sem("picked"), 1)
                                    for q in range(HU):
                                        dve.wait_ge(sem(f"sw_g{s - HU + 1 + q}"), (gathered + i + 1) * 16)
                                    dve.wait_ge(sem("picked"), (half + CREDIT) * 3 + 3)
                                    v.tensor_tensor(LG[:, chunks, :], summed[:], ga[:, s - HU + 1:s + 1, :], ALU.add).then_inc(sem("logits"), 1)
                    clear_semaphores()

                with ExitStack() as pctx:
                    pen = sb(pctx, "pen", [P, NC1])
                    most = sb(pctx, "most", [P, NH])
                    diag = sb(pctx, "diag", [P, NH])
                    total = sb(pctx, "total", [P, NH])
                    ps_t = ps(pctx, "ps_t", [P, P])
                    ps_m = ps(pctx, "ps_m", [P, NH])
                    ps_z = ps(pctx, "ps_z", [P, NH])
                    with nc.Block() as block:
                        @block.vector
                        def _(dve):
                            v, step = nc.vector, Chain(dve, sem("chain"))
                            v.tensor_scalar(pen[:], meta[:, :, 0], 0.0, -NEG, ALU.min, ALU.mult)
                            step(v.scalar_tensor_tensor(LG[:], LG[:], 0.2, LG[:], ALU.mult, ALU.max))
                            step(v.tensor_tensor(LG[:], LG[:], pen[:].unsqueeze(2).to_broadcast([P, NC1, NH]), ALU.add))
                            v.tensor_reduce(most[:], LG[:].rearrange("p n h -> p h n"), AX.X, ALU.max).then_inc(sem("most"), 1)
                            dve.wait_ge(sem("turned"), 1)
                            step(v.tensor_reduce(diag[0:NH, 0:1], ps_t[0:NH, :], AX.X, ALU.max))
                            v.tensor_scalar(total[0:NH, :], ident[0:NH, 0:NH], diag[0:NH, 0:1], None, ALU.mult).then_inc(sem("diag"), 1)
                            dve.wait_ge(sem("spread"), 1)
                            v.tensor_tensor(LG[:], LG[:], ps_m[:].unsqueeze(1).to_broadcast([P, NC1, NH]), ALU.subtract).then_inc(sem("shifted"), 1)
                            dve.wait_ge(sem("exp"), 1)
                            v.tensor_reduce(most[:], LG[:].rearrange("p n h -> p h n"), AX.X, ALU.add).then_inc(sem("sums"), 1)
                            dve.wait_ge(sem("z"), 1)
                            step(v.reciprocal(diag[:], ps_z[:]))
                            step(v.tensor_tensor(LG[:], LG[:], diag[:].unsqueeze(1).to_broadcast([P, NC1, NH]), ALU.mult))

                        @block.tensor
                        def _(pe):
                            t_ = nc.tensor
                            pe.wait_ge(sem("most"), 1)
                            t_.transpose(ps_t[0:NH, :], most[:], ident[:]).then_inc(sem("turned"), 1)
                            pe.wait_ge(sem("diag"), 1)
                            t_.matmul(ps_m[:], ones[0:NH, :], total[0:NH, :], start=True, stop=True).then_inc(sem("spread"), 1)
                            pe.wait_ge(sem("sums"), 1)
                            t_.matmul(ps_z[:], ones[:], most[:], start=True, stop=True).then_inc(sem("z"), 1)

                        @block.scalar
                        def _(act):
                            act.wait_ge(sem("shifted"), 1)
                            nc.scalar.activation(LG[:], LG[:], ACT.Exp).then_inc(sem("exp"), 1)
                    clear_semaphores()

                with ExitStack() as pctx:
                    gathered2 = 5 * TURNS1
                    G = sb(pctx, "G", [P, U, D])
                    msg = sb(pctx, "msg", [P, RING, D])
                    hot = sb(pctx, "hotm", [P, RING, P])
                    dist = sb(pctx, "dist", [P, 2, P])
                    ps_a = [ps(pctx, f"ps_a{b}", [P, D]) for b in range(BANKS)]
                    with nc.Block() as block:
                        @block.sync
                        def _(sp):
                            with nc.sync.Fori(0, TURNS1) as i:
                                for q in range(U // QU):
                                    load_indices(sp, 1, i, q, ixs, "msg")

                        @block.gpsimd
                        def _(pool):
                            gather_rows(pool, TURNS1, rel_d, ixs, G, "msg")

                        @block.tensor
                        def _(pe):
                            credit(pe, "agg")
                            for (c3,) in walk(nc.tensor, TURNS1, 3):
                                if c3:
                                    n, i, s = c3
                                    pe.wait_ge(sem("msg"), upto(n))
                                    pe.wait_ge(sem("hot"), upto(n))
                                    pe.wait_ge(sem("acc"), upto(n - BANKS))
                                    nc.tensor.matmul(ps_a[s % BANKS][:], hot[:, s % RING, :], msg[:, s % RING, :],
                                                     start=True, stop=True).then_inc(sem("agg"), 1)

                        @block.scalar
                        def _(act):
                            credit(act, "dist", "hot")
                            for c0, c1 in walk(nc.scalar, TURNS1, 0, 1):
                                if c0:
                                    one_hot_distance(act, c0, meta[:, ds(c0[0]), 0], dist)
                                if c1:
                                    n, i, s = c1
                                    act.wait_ge(sem("agg"), upto(n - RING))
                                    one_hot_row(act, c1, dist, hot[:, s % RING, :])

                        @block.vector
                        def _(dve):
                            v = nc.vector
                            credit(dve, "msg", "acc")
                            bucket = Buckets(nc, mybir.EngineType.DVE, bmap[0:1, 1, :], T - 1, 4)
                            for c0, c4 in walk(nc.vector, TURNS1, 0, 4):
                                if c0:
                                    n, i, s = c0
                                    dve.wait_ge(sem("agg"), upto(n - RING))
                                    dve.wait_ge(sem(f"sw_g{s}"), (gathered2 + i + 1) * 16)
                                    v.tensor_tensor(msg[:, s % RING, :].rearrange("p (h d) -> p h d", h=NH),
                                                    G[:, s, :].rearrange("p (h d) -> p h d", h=NH),
                                                    LG[:, ds(n), :].rearrange("p t h -> p (t h)").unsqueeze(2).to_broadcast([P, NH, HD]),
                                                    ALU.mult).then_inc(sem("msg"), 1)
                                if c4:
                                    n, i, s = c4
                                    b = bucket(c4)
                                    dve.wait_ge(sem("agg"), upto(n))
                                    dve.wait_ge(sem("acc"), upto(n - 1))
                                    to = X[:, ds(b), :]
                                    v.tensor_tensor(to, ps_a[s % BANKS][:].unsqueeze(1), to, ALU.add).then_inc(sem("acc"), 1)
                    clear_semaphores()

        def distance_attention():
            gathered = [6 * TURNS1 * 16 if s < U else 0 for s in range(U3)]
            H1 = HD + 1
            D1 = NH * H1
            FC = D1 + NH
            WC = D1 + 2 * NH
            acc3 = arena[:, 0:T * D1].rearrange("p (t c) -> p t c", t=T)
            ctx = ExitStack()
            with ctx:
                ixs = sb(ctx, "ixs", [P, U3], I32)
                ew = sb(ctx, "ew", [P, NC2, NH])
                asT = sb(ctx, "asT", [P, T, NH])
                awe = sb(ctx, "awe", [P, NH])
                ab = sb(ctx, "ab", [P, NH])
                with ExitStack() as pctx:
                    W3 = sb(pctx, "W3", [P, DH + 1, WC])
                    aw = sb(pctx, "aw", [P, 2, D])
                    scratch = sb(pctx, "scratch", [P, DH + 1, D])
                    cur = sb(pctx, "cur", [P, TG, D])
                    stage = sb(pctx, "stage", [P, TG, WC])
                    ps_f = [ps(pctx, f"ps_f{b}", [P, WC]) for b in range(TG)]
                    with nc.Block() as block:
                        @block.sync
                        def _(sp):
                            for h in range(DH):
                                sp.dma_start(W3[:, h, 0:D1].rearrange("p (k d) -> p k d", k=NH)[:, :, 0:HD],
                                             L3_gnn_Ws[:, h * P:(h + 1) * P, :].rearrange("k p d -> p k d")).then_inc(sem("w_in"), 16)
                            for k in range(NH):
                                sp.dma_start(W3[:, DH, k * H1:k * H1 + HD], L3_gnn_bs[k:k + 1, :].to_broadcast([P, HD])).then_inc(sem("w_in"), 16)
                            for m, at in enumerate((HD, 0)):
                                for k in range(NH):
                                    sp.dma_start(aw[:, m, k * HD:(k + 1) * HD],
                                                 L3_gnn_aw[k:k + 1, at:at + HD].to_broadcast([P, HD])).then_inc(sem("w_in"), 16)
                            for k in range(NH):
                                sp.dma_start(awe[:, k:k + 1], L3_gnn_aw[k:k + 1, 2 * HD:2 * HD + 1].to_broadcast([P, 1])).then_inc(sem("w_in"), 16)
                            sp.dma_start(ab[:], L3_gnn_ab.rearrange("(a d) -> a d", a=1).to_broadcast([P, NH])).then_inc(sem("w_in"), 16)

                        @block.vector
                        def _(dve):
                            v, step = nc.vector, Chain(dve, sem("chain"))
                            v.memset(acc3, 0.0)
                            v.memset(W3[:, 0:DH, 0:D1].rearrange("p j (k d) -> p j k d", k=NH)[:, :, :, HD:H1], 0.0)
                            v.memset(W3[:, DH, 0:D1].rearrange("p (k d) -> p k d", k=NH)[:, :, HD:H1], 1.0)
                            dve.wait_ge(sem("w_in"), 16 * (DH + 1 + 4 * NH))
                            v.tensor_copy(idx[:, 1, 0:NC2], meta2[:, :, 1])
                            for m in range(2):
                                for j in range(DH + 1):
                                    last = v.tensor_tensor(scratch[:, j, :].rearrange("p (k d) -> p k d", k=NH),
                                                           W3[:, j, 0:D1].rearrange("p (k d) -> p k d", k=NH)[:, :, 0:HD],
                                                           aw[:, m, :].rearrange("p (k d) -> p k d", k=NH), ALU.mult)
                                step(last)
                                step(v.tensor_reduce(W3[:, :, D1 + m * NH:D1 + (m + 1) * NH],
                                                     scratch[:].rearrange("p k (h d) -> p k h d", h=NH), AX.X, ALU.add))
                            v.tensor_tensor(ew[:], meta2[:, :, 2].unsqueeze(2).to_broadcast([P, NC2, NH]),
                                            awe[:].unsqueeze(1).to_broadcast([P, NC2, NH]), ALU.mult)
                            step(v.tensor_tensor(W3[:, DH, D1 + NH:WC], W3[:, DH, D1 + NH:WC], ab[:], ALU.add))
                    clear_semaphores()
                    with nc.Block() as block:
                        @block.tensor
                        def _(pe):
                            credit(pe, "rows")
                            for (c0,) in walk(nc.tensor, T // TG, 0, width=TG):
                                if not c0:
                                    continue
                                t, i, s = c0
                                pe.wait_ge(sem("cur"), upto(t))
                                pe.wait_ge(sem("staged"), upto(t - TG))
                                for h in range(DH):
                                    last = nc.tensor.matmul(ps_f[s][:], cur[:, s, h * P:(h + 1) * P], W3[:, h, :],
                                                            start=(h == 0), stop=(h == DH - 1))
                                last.then_inc(sem("rows"), 1)

                        @block.scalar
                        def _(act):
                            credit(act, "cur")
                            for (c0,) in walk(nc.scalar, T // TG, 0, width=TG):
                                if not c0:
                                    continue
                                t, i, s = c0
                                wait_ahead(act, (sem("rows"), upto(t - TG)))
                                nc.scalar.copy(cur[:, s, :], hT[:, ds(t), :, :].rearrange("p t h n -> p (t h n)")).then_inc(sem("cur"), 1)

                        @block.vector
                        def _(dve):
                            v = nc.vector
                            credit(dve, "staged", "as")
                            for c0, c1 in walk(nc.vector, T // TG, 0, 1, width=TG):
                                if c0:
                                    t, i, s = c0
                                    dve.wait_ge(sem("rows"), upto(t))
                                    if not isinstance(i, int):
                                        dve.wait_ge(sem(f"feat_out{s}"), i * 16)
                                    v.tensor_tensor(stage[:, s, :], ps_f[s][:], W3[:, DH, :], ALU.add).then_inc(sem("staged"), 1)
                                if c1:
                                    t, i, s = c1
                                    dve.wait_ge(sem("staged"), upto(t))
                                    v.tensor_copy(asT[:, ds(t), :], stage[:, s:s + 1, FC:WC]).then_inc(sem("as"), 1)

                        @block.sync
                        def _(sp):
                            with nc.sync.Fori(0, T // TG) as i:
                                for s in range(TG):
                                    t = i * TG + s
                                    sp.wait_ge(sem("staged"), upto(t))
                                    sp.dma_start(feat_d[ds(t * P, P), :], stage[:, s, 0:FC]).then_inc(sem(f"feat_out{s}"), 16)
                            for s in range(TG):
                                sp.wait_ge(sem(f"feat_out{s}"), 16 * (T // TG))
                    clear_semaphores()

                with ExitStack() as pctx:
                    G = sb(pctx, "G", [P, U3, FC])
                    hot = sb(pctx, "hotm", [P, U3, P])
                    hotT = sb(pctx, "hotT", [P, 4, P])
                    dist = sb(pctx, "dist", [P, 2, P])
                    own = sb(pctx, "own", [P, U3, NH])
                    score = sb(pctx, "score", [P, 2, Q3, NH])
                    w = sb(pctx, "w", [P, U3, NH])
                    msg = sb(pctx, "msg", [P, 4, D1])
                    ps_t = [ps(pctx, f"ps_t{b}", [P, P]) for b in range(2)]
                    ps_s = [ps(pctx, f"ps_s{b}", [P, Q3, NH]) for b in range(2)]
                    ps_a = [ps(pctx, f"ps_a{b}", [P, D1]) for b in range(4)]
                    BATCHES = U3 // Q3
                    with nc.Block() as block:
                        @block.sync
                        def _(sp):
                            bucket = Buckets(nc, mybir.EngineType.SP, bmap[0:1, 2, :], T - 1, 0, width=U3, part=Q3)
                            with nc.sync.Fori(0, TURNS2) as i:
                                for q in range(BATCHES):
                                    sp.wait_ge(sem("as_e"), upto(i * U3 + q * Q3 + Q3 - 1 - U3))
                                    for s in range(q * Q3, (q + 1) * Q3):
                                        b = bucket((i * U3 + s, i, s))
                                        sp.dma_start(own[:, s:s + 1, :], asT[:, ds(b), :]).then_inc(sem(f"own_in{q}"), 16)
                                    load_indices(sp, 1, i, q, ixs, "msg", width=U3, part=Q3)

                        @block.gpsimd
                        def _(pool):
                            gather_rows(pool, TURNS2, feat_d, ixs, G, "msg", width=U3, part=Q3)

                        @block.tensor
                        def _(pe):
                            t_ = nc.tensor
                            credit(pe, "hotT", "as_e", "agg")
                            for c0, c1_, c9 in walk(nc.tensor, TURNS2, 0, 1, 9, width=U3):
                                if c0:
                                    n, i, s = c0
                                    pe.wait_ge(sem("hot"), upto(n))
                                    pe.wait_ge(sem("hotT_sb"), upto(n - 2))
                                    t_.transpose(ps_t[s % 2][:], hot[:, s, :], ident[:]).then_inc(sem("hotT"), 1)
                                if c1_:
                                    n, i, s = c1_
                                    batch = i * BATCHES + s // Q3
                                    pe.wait_ge(sem("hotT_sb"), upto(n))
                                    if s % Q3 == 0:
                                        pe.wait_ge(sem(f"own_in{s // Q3}"), (i + 1) * Q3 * 16)
                                        pe.wait_ge(sem("taken"), upto(batch - 2))
                                    t_.matmul(ps_s[s // Q3 % 2][:, s % Q3, :], hotT[:, s % 4, :],
                                              own[:, s, :], start=True, stop=True).then_inc(sem("as_e"), 1)
                                if c9:
                                    n, i, s = c9
                                    pe.wait_ge(sem("msg"), upto(n))
                                    pe.wait_ge(sem("acc"), upto(n - 4))
                                    t_.matmul(ps_a[s % 4][:], hot[:, s, :], msg[:, s % 4, :], start=True, stop=True).then_inc(sem("agg"), 1)

                        @block.scalar
                        def _(act):
                            credit(act, "hotT_sb", "bounded", "w", "dist", "hot")
                            for c0, c1, c2, c5 in walk(nc.scalar, TURNS2, 0, 1, 2, 5, width=U3):
                                if c0:
                                    n, i, s = c0
                                    one_hot_distance(act, c0, meta2[:, ds(n), 0], dist)
                                if c1:
                                    n, i, s = c1
                                    act.wait_ge(sem("agg"), upto(n - U3))
                                    one_hot_row(act, c1, dist, hot[:, s, :])
                                if c2:
                                    n, i, s = c2
                                    act.wait_ge(sem("hotT"), upto(n))
                                    act.wait_ge(sem("as_e"), upto(n - 4))
                                    nc.scalar.copy(hotT[:, s % 4, :], ps_t[s % 2][:]).then_inc(sem("hotT_sb"), 1)
                                if c5 and c5[2] % Q3 == Q3 - 1:
                                    n, i, s = c5
                                    batch = i * BATCHES + s // Q3
                                    sc = score[:, s // Q3 % 2, :, :]
                                    act.wait_ge(sem("scored"), upto(batch))
                                    nc.scalar.activation(sc, sc, ACT.Relu).then_inc(sem("bounded"), 1)
                                    act.wait_ge(sem("msg"), upto(n - U3))
                                    act.wait_ge(sem("bounded"), upto(batch))
                                    nc.scalar.activation(w[:, s - Q3 + 1:s + 1, :], sc, ACT.Exp, scale=-1.0 / 20.0).then_inc(sem("w"), 1)

                        @block.vector
                        def _(dve):
                            v = nc.vector
                            credit(dve, "taken", "scored", "msg", "acc")
                            bucket = Buckets(nc, mybir.EngineType.DVE, bmap[0:1, 2, :], T - 1, 12, width=U3, part=Q3)
                            for c2_, c7, c12 in walk(nc.vector, TURNS2, 2, 7, 12, width=U3):
                                if c12:
                                    n, i, s = c12
                                    b = bucket(c12)
                                    dve.wait_ge(sem("agg"), upto(n))
                                    dve.wait_ge(sem("acc"), upto(n - 1))
                                    to = acc3[:, ds(b), :]
                                    v.tensor_tensor(to, ps_a[s % 4][:].unsqueeze(1), to, ALU.add).then_inc(sem("acc"), 1)
                                if c2_ and c2_[2] % Q3 == Q3 - 1:
                                    n, i, s = c2_
                                    batch = i * BATCHES + s // Q3
                                    sc = score[:, s // Q3 % 2, :, :]
                                    dve.wait_ge(sem("w"), upto(batch - 2))
                                    dve.wait_ge(sem("as_e"), upto(n))
                                    v.tensor_tensor(sc, ps_s[s // Q3 % 2][:], ew[:, ds(n - (Q3 - 1), Q3), :], ALU.add).then_inc(sem("taken"), 1)
                                    for q in range(s - Q3 + 1, s + 1):
                                        dve.wait_ge(sem(f"sw_g{q}"), gathered[q] + (i + 1) * 16)
                                    dve.wait_ge(sem("taken"), upto(batch))
                                    v.tensor_tensor(sc, sc, G[:, s - Q3 + 1:s + 1, D1:FC], ALU.add).then_inc(sem("scored"), 1)
                                if c7:
                                    n, i, s = c7
                                    if s % Q3 == 0:
                                        dve.wait_ge(sem("w"), upto(i * BATCHES + s // Q3))
                                    dve.wait_ge(sem("agg"), upto(n - 4))
                                    v.tensor_tensor(msg[:, s % 4, :].rearrange("p (h d) -> p h d", h=NH),
                                                    G[:, s, 0:D1].rearrange("p (h d) -> p h d", h=NH),
                                                    w[:, s, :].unsqueeze(2).to_broadcast([P, NH, H1]),
                                                    ALU.mult).then_inc(sem("msg"), 1)
                    clear_semaphores()

                with nc.Block() as block:
                    PIECES = 4
                    TP = (T - 1) // PIECES

                    @block.vector
                    def _(dve):
                        v, step = nc.vector, Chain(dve, sem("chain"))
                        for k in range(NH):
                            one = acc3[:, :, k * H1 + HD:(k + 1) * H1]
                            last = v.reciprocal(one, one)
                        step(last)
                        for q in range(PIECES + 1):
                            at, parts = (slice(q * TP, (q + 1) * TP), P) if q < PIECES else (slice(T - 1, T), NLAST)
                            nt = at.stop - at.start
                            heads = [acc3[0:parts, at, k * H1:k * H1 + HD] for k in range(NH)]
                            for k in range(NH):
                                last = v.tensor_tensor(heads[k], heads[k], acc3[0:parts, at, k * H1 + HD:(k + 1) * H1].to_broadcast(
                                    [parts, nt, HD]), ALU.mult)
                            step(last)
                            for k in range(NH):
                                rows = X[0:parts, at, k * HD:(k + 1) * HD]
                                last = v.tensor_tensor(rows, rows, heads[k], ALU.add)
                            last.then_inc(sem("x"), 1)

                    @block.sync
                    def _(sp):
                        for q in range(PIECES):
                            sp.wait_ge(sem("x"), q + 1)
                            sp.dma_start(out[q * TP * P:(q + 1) * TP * P, :].rearrange("(t p) d -> p t d", p=P),
                                         X[:, q * TP:(q + 1) * TP, :]).then_inc(sem("out"), 16)
                        sp.wait_ge(sem("x"), PIECES + 1)
                        sp.dma_start(out[(T - 1) * P:N, :], X[0:NLAST, T - 1, :]).then_inc(sem("out"), 16)
                        sp.wait_ge(sem("out"), 16 * (PIECES + 1))

        sort_edges()
        normalize(load_meta=True)
        rgcn()
        normalize(keep=True)
        gated()
        normalize(early=[(W_in, L2_gnn_W.rearrange("r (h p) d -> p r h d", p=P))])
        relational_attention()
        normalize(early=[(meta2, rec2_d[0:NC2 * P, :].rearrange("(j p) w -> p j w", p=P))])
        distance_attention()


_INS = ["x", "src", "dst", "edge_attr_32", "edge_attr_64", "edge_type_3", "edge_type_8", "edge_weight",
        "L0_gnn_W", "L0_gnn_root", "L0_gnn_bias", "L0_gnn_nn_w", "L0_gnn_nn_b",
        "L1_gnn_W1", "L1_gnn_b1", "L1_gnn_W2", "L1_gnn_b2", "L1_gnn_U1", "L1_gnn_c1", "L1_gnn_U2", "L1_gnn_c2",
        "L2_gnn_W", "L2_gnn_a_src", "L2_gnn_a_dst", "L3_gnn_Ws", "L3_gnn_bs", "L3_gnn_aw", "L3_gnn_ab"]


def kernel(**inputs):
    import numpy as np
    import concourse.bacc as bacc
    from concourse.bass_utils import run_bass_kernel_spmd

    nc = bacc.Bacc("TRN2", target_bir_lowering=False, num_devices=1)
    arrays, args = {}, []
    for name in _INS:
        arrays[name] = np.ascontiguousarray(inputs[name])
        args.append(nc.dram_tensor(name, arrays[name].shape, mybir.dt.from_np(arrays[name].dtype), kind="ExternalInput").ap())
    args.append(nc.dram_tensor("out", (N, D), F32, kind="ExternalOutput").ap())
    build(nc, *args)
    r = run_bass_kernel_spmd(nc, [arrays], core_ids=[0])
    return r.results[0]["out"]
```
